# Optimizing a Trainium2 kernel written in Bass

```python
import numpy as np
import jax
import jax.numpy as jnp

def _softmax(x, axis=-1):
    return jax.nn.softmax(x, axis=axis)

def _gelu(x):
    return jax.nn.gelu(x, approximate=True)

def _silu(x):
    return jax.nn.silu(x)

def _sigmoid(x):
    return jax.nn.sigmoid(x)

def _layernorm(x, axis=-1, eps=1e-05):
    m = jnp.mean(x, axis=axis, keepdims=True)
    v = jnp.var(x, axis=axis, keepdims=True)
    return (x - m) / jnp.sqrt(v + eps)

def _scatter_add(tgt, idx, src, axis=0):
    return tgt.at[idx].add(src)

def _segment_sum(src, seg, n):
    return jax.ops.segment_sum(src, seg, n)
kernel_name = 'mk_seq_postln_d1_jaxref_r8_0838ae'

def setup_inputs(seed: int=0):
    np.random.seed(seed)
    _w = jnp.asarray

    def _L0_attn_setup():
        import jax, jax.numpy as jnp
        import numpy as np
        MAX_LR = 0.01
        NS_A, NS_B, NS_C = (3.4445, -4.775, 2.0315)

        def newtonschulz5(G, steps=5, eps=1e-07):
            transpose = G.shape[-2] > G.shape[-1]
            X = jnp.swapaxes(G, -2, -1) if transpose else G
            X = X / (jnp.linalg.norm(X, axis=(-2, -1), keepdims=True) + eps)
            for _ in range(steps):
                A = X @ jnp.swapaxes(X, -2, -1)
                Bm = NS_B * A + NS_C * (A @ A)
                X = NS_A * X + Bm @ X
            return jnp.swapaxes(X, -2, -1) if transpose else X

        def _reference_tuple_inner(tokens, wq, wk, wv, wo, w_lr, w_target, w_gates, rms_w):
            N = tokens.shape[1]
            scale = wq.shape[-1] ** (-0.5)
            eps = jnp.finfo(tokens.dtype).eps
            t = tokens * jax.lax.rsqrt(jnp.mean(tokens * tokens, -1, keepdims=True) + eps) * rms_w
            gates = jnp.swapaxes(jax.nn.sigmoid(t @ w_gates), -2, -1)[..., None]
            q = jnp.einsum('bnd,hde->bhne', t, wq)
            k = jnp.einsum('bnd,hde->bhne', t, wk)
            v = jnp.einsum('bnd,hde->bhne', t, wv)
            score = jnp.einsum('bhie,bhje->bhij', q, k) * scale
            causal_mask = jnp.triu(jnp.ones((N, N), bool), 1)
            score = jnp.where(causal_mask, -jnp.finfo(score.dtype).max, score)
            attn = jax.nn.softmax(score, axis=-1)
            out = jnp.einsum('bhij,bhje->bhie', attn, v) * gates
            pred_values = jnp.einsum('bhne,hed->bnd', out, wo)
            tv = t[:, 1:] @ w_target
            tv = (tv - tv.mean(-1, keepdims=True)) * jax.lax.rsqrt(tv.var(-1, keepdims=True) + 1e-05)
            ts = t[:, :-1]
            pv = pred_values[:, :-1]
            o = out[:, :, :-1]
            g = gates[:, :, :-1]
            a = attn[:, :, :-1, :-1]
            qs, ks_, vs = (q[:, :, :-1], k[:, :, :-1], v[:, :, :-1])
            lrs = jax.nn.sigmoid(ts @ w_lr) * MAX_LR
            lr, mlr = (lrs[..., 0], lrs[..., 1])
            error = tv - pv
            dout = jnp.einsum('bnd,hed->bhne', error, wo)
            du = dout * g
            delta = jnp.sum(dout * o, -1, keepdims=True)
            dv = jnp.einsum('bhij,bhie->bhje', a, du)
            dattn = jnp.einsum('bhje,bhie->bhij', vs, du)
            dscore = scale * a * (dattn - delta)
            dq = jnp.einsum('bhje,bhij->bhie', ks_, dscore)
            dk = jnp.einsum('bhie,bhij->bhje', qs, dscore)
            t_qk = ts * lr[..., None]
            t_v = ts * mlr[..., None]
            o_wo = o * mlr[:, None, :, None]
            dwq = jnp.einsum('bhie,bid->bhde', dq, t_qk)
            dwk = jnp.einsum('bhje,bjd->bhde', dk, t_qk)
            dwv = jnp.einsum('bhje,bjd->bhde', dv, t_v)
            dwo = jnp.einsum('bnd,bhne->bhed', error, o_wo)
            dwv = newtonschulz5(dwv)
            dwo = newtonschulz5(dwo)
            return (pred_values, dwq, dwk, dwv, dwo)
        key = jax.random.key(seed)
        ks = jax.random.split(key, 9)
        B, N, D, H, DH = (4, 128, 128, 8, 64)
        s = D ** (-0.5)
        return {'tokens': jax.random.normal(ks[0], (B, N, D), jnp.float32), 'wq': jax.random.normal(ks[1], (H, D, DH), jnp.float32) * s, 'wk': jax.random.normal(ks[2], (H, D, DH), jnp.float32) * s, 'wv': jax.random.normal(ks[3], (H, D, DH), jnp.float32) * s, 'wo': jax.random.normal(ks[4], (H, DH, D), jnp.float32) * s, 'w_lr': jax.random.normal(ks[5], (D, 2), jnp.float32) * 0.02, 'w_target': jax.random.normal(ks[6], (D, D), jnp.float32) * 0.02, 'w_gates': jax.random.normal(ks[7], (D, H), jnp.float32) * 0.02, 'rms_w': jnp.ones((D,), jnp.float32)}
    _L0_attn_in = _L0_attn_setup()

    def _L0_ffn_setup():
        import jax, jax.numpy as jnp
        import numpy as np
        B, T, D = (2, 128, 128)
        E = 16
        H = 256
        K = 2
        HS = H * 2
        key = jax.random.key(seed)
        ks = jax.random.split(key, 16)
        s = 0.02
        f32 = jnp.float32
        return {'x': jax.random.normal(ks[0], (B, T, D), f32), 'Wg': jax.random.normal(ks[1], (D, E), f32) * s, 'W1': jax.random.normal(ks[2], (E, D, H), f32) * s, 'b1': jax.random.normal(ks[3], (E, H), f32) * s, 'W11': jax.random.normal(ks[4], (E, D, H), f32) * s, 'b11': jax.random.normal(ks[5], (E, H), f32) * s, 'W2': jax.random.normal(ks[6], (E, H, D), f32) * s, 'b2': jax.random.normal(ks[7], (E, D), f32) * s, 'Ws1': jax.random.normal(ks[8], (D, HS), f32) * s, 'bs1': jax.random.normal(ks[9], (HS,), f32) * s, 'Ws11': jax.random.normal(ks[10], (D, HS), f32) * s, 'bs11': jax.random.normal(ks[11], (HS,), f32) * s, 'Ws2': jax.random.normal(ks[12], (HS, D), f32) * s, 'bs2': jax.random.normal(ks[13], (D,), f32) * s}
    _L0_ffn_in = _L0_ffn_setup()
    _d = {'L0_attn_tokens': _L0_attn_in['tokens'], 'L0_attn_wq': _L0_attn_in['wq'], 'L0_attn_wk': _L0_attn_in['wk'], 'L0_attn_wv': _L0_attn_in['wv'], 'L0_attn_wo': _L0_attn_in['wo'], 'L0_attn_w_lr': _L0_attn_in['w_lr'], 'L0_attn_w_target': _L0_attn_in['w_target'], 'L0_attn_w_gates': _L0_attn_in['w_gates'], 'L0_attn_rms_w': _L0_attn_in['rms_w'], 'L0_ffn_Wg': _L0_ffn_in['Wg'], 'L0_ffn_W1': _L0_ffn_in['W1'], 'L0_ffn_b1': _L0_ffn_in['b1'], 'L0_ffn_W11': _L0_ffn_in['W11'], 'L0_ffn_b11': _L0_ffn_in['b11'], 'L0_ffn_W2': _L0_ffn_in['W2'], 'L0_ffn_b2': _L0_ffn_in['b2'], 'L0_ffn_Ws1': _L0_ffn_in['Ws1'], 'L0_ffn_bs1': _L0_ffn_in['bs1'], 'L0_ffn_Ws11': _L0_ffn_in['Ws11'], 'L0_ffn_bs11': _L0_ffn_in['bs11'], 'L0_ffn_Ws2': _L0_ffn_in['Ws2'], 'L0_ffn_bs2': _L0_ffn_in['bs2']}
    _x0 = _d['L0_attn_tokens']
    _d['L0_attn_tokens'] = jax.random.normal(jax.random.fold_in(jax.random.key(seed), 1), (1, 2048, 128), dtype=_x0.dtype)
    del _x0
    return _d

def reference(L0_attn_tokens, L0_attn_wq, L0_attn_wk, L0_attn_wv, L0_attn_wo, L0_attn_w_lr, L0_attn_w_target, L0_attn_w_gates, L0_attn_rms_w, L0_ffn_Wg, L0_ffn_W1, L0_ffn_b1, L0_ffn_W11, L0_ffn_b11, L0_ffn_W2, L0_ffn_b2, L0_ffn_Ws1, L0_ffn_bs1, L0_ffn_Ws11, L0_ffn_bs11, L0_ffn_Ws2, L0_ffn_bs2):

    def _L0_attn_ref(tokens, wq, wk, wv, wo, w_lr, w_target, w_gates, rms_w):
        import jax, jax.numpy as jnp
        import numpy as np
        MAX_LR = 0.01
        NS_A, NS_B, NS_C = (3.4445, -4.775, 2.0315)

        def newtonschulz5(G, steps=5, eps=1e-07):
            transpose = G.shape[-2] > G.shape[-1]
            X = jnp.swapaxes(G, -2, -1) if transpose else G
            X = X / (jnp.linalg.norm(X, axis=(-2, -1), keepdims=True) + eps)
            for _ in range(steps):
                A = X @ jnp.swapaxes(X, -2, -1)
                Bm = NS_B * A + NS_C * (A @ A)
                X = NS_A * X + Bm @ X
            return jnp.swapaxes(X, -2, -1) if transpose else X

        def _reference_tuple_inner(tokens, wq, wk, wv, wo, w_lr, w_target, w_gates, rms_w):
            N = tokens.shape[1]
            scale = wq.shape[-1] ** (-0.5)
            eps = jnp.finfo(tokens.dtype).eps
            t = tokens * jax.lax.rsqrt(jnp.mean(tokens * tokens, -1, keepdims=True) + eps) * rms_w
            gates = jnp.swapaxes(jax.nn.sigmoid(t @ w_gates), -2, -1)[..., None]
            q = jnp.einsum('bnd,hde->bhne', t, wq)
            k = jnp.einsum('bnd,hde->bhne', t, wk)
            v = jnp.einsum('bnd,hde->bhne', t, wv)
            score = jnp.einsum('bhie,bhje->bhij', q, k) * scale
            causal_mask = jnp.triu(jnp.ones((N, N), bool), 1)
            score = jnp.where(causal_mask, -jnp.finfo(score.dtype).max, score)
            attn = jax.nn.softmax(score, axis=-1)
            out = jnp.einsum('bhij,bhje->bhie', attn, v) * gates
            pred_values = jnp.einsum('bhne,hed->bnd', out, wo)
            tv = t[:, 1:] @ w_target
            tv = (tv - tv.mean(-1, keepdims=True)) * jax.lax.rsqrt(tv.var(-1, keepdims=True) + 1e-05)
            ts = t[:, :-1]
            pv = pred_values[:, :-1]
            o = out[:, :, :-1]
            g = gates[:, :, :-1]
            a = attn[:, :, :-1, :-1]
            qs, ks_, vs = (q[:, :, :-1], k[:, :, :-1], v[:, :, :-1])
            lrs = jax.nn.sigmoid(ts @ w_lr) * MAX_LR
            lr, mlr = (lrs[..., 0], lrs[..., 1])
            error = tv - pv
            dout = jnp.einsum('bnd,hed->bhne', error, wo)
            du = dout * g
            delta = jnp.sum(dout * o, -1, keepdims=True)
            dv = jnp.einsum('bhij,bhie->bhje', a, du)
            dattn = jnp.einsum('bhje,bhie->bhij', vs, du)
            dscore = scale * a * (dattn - delta)
            dq = jnp.einsum('bhje,bhij->bhie', ks_, dscore)
            dk = jnp.einsum('bhie,bhij->bhje', qs, dscore)
            t_qk = ts * lr[..., None]
            t_v = ts * mlr[..., None]
            o_wo = o * mlr[:, None, :, None]
            dwq = jnp.einsum('bhie,bid->bhde', dq, t_qk)
            dwk = jnp.einsum('bhje,bjd->bhde', dk, t_qk)
            dwv = jnp.einsum('bhje,bjd->bhde', dv, t_v)
            dwo = jnp.einsum('bnd,bhne->bhed', error, o_wo)
            dwv = newtonschulz5(dwv)
            dwo = newtonschulz5(dwo)
            return (pred_values, dwq, dwk, dwv, dwo)
        return _reference_tuple_inner(tokens, wq, wk, wv, wo, w_lr, w_target, w_gates, rms_w)[0]

    def _L0_ffn_ref(x, Wg, W1, b1, W11, b11, W2, b2, Ws1, bs1, Ws11, bs11, Ws2, bs2):
        import jax, jax.numpy as jnp
        import numpy as np
        B, T, D = (2, 128, 128)
        E = 16
        H = 256
        K = 2
        HS = H * 2
        b, t, d = x.shape
        xf = x.reshape(b * t, d)
        n = xf.shape[0]
        logits = xf @ Wg
        _, topi = jax.lax.top_k(logits, K)
        mask = jnp.zeros((n, E), bool).at[jnp.arange(n)[:, None], topi].set(True)
        gates = jax.nn.softmax(jnp.where(mask, logits, -jnp.inf), axis=-1)
        y = jnp.zeros_like(xf)
        for e in range(E):
            h = jax.nn.silu(xf @ W1[e] + b1[e]) * (xf @ W11[e] + b11[e])
            y = y + (h @ W2[e] + b2[e]) * gates[:, e, None]
        z = jax.nn.silu(xf @ Ws1 + bs1) * (xf @ Ws11 + bs11) @ Ws2 + bs2
        return (y + z).reshape(b, t, d)
    x = L0_attn_tokens
    x = _layernorm(x + _L0_attn_ref(x, L0_attn_wq, L0_attn_wk, L0_attn_wv, L0_attn_wo, L0_attn_w_lr, L0_attn_w_target, L0_attn_w_gates, L0_attn_rms_w), axis=-1)
    x = _layernorm(x + _L0_ffn_ref(x, L0_ffn_Wg, L0_ffn_W1, L0_ffn_b1, L0_ffn_W11, L0_ffn_b11, L0_ffn_W2, L0_ffn_b2, L0_ffn_Ws1, L0_ffn_bs1, L0_ffn_Ws11, L0_ffn_bs11, L0_ffn_Ws2, L0_ffn_bs2), axis=-1)
    return x

_drawn_inputs = setup_inputs


def setup_inputs(seed=0):
    import zlib

    import numpy as np

    out = dict(_drawn_inputs(seed))
    spreads = {'L0_attn_rms_w': (1.0, 0.2)}
    factors = {'L0_attn_w_gates': 3.623,
     'L0_ffn_Wg': 3.939,
     'L0_ffn_W1': 8.0,
     'L0_ffn_b1': 8.0,
     'L0_ffn_W11': 8.0,
     'L0_ffn_b11': 8.0,
     'L0_ffn_W2': 8.0,
     'L0_ffn_b2': 16.855,
     'L0_ffn_Ws1': 4.847,
     'L0_ffn_bs1': 8.0,
     'L0_ffn_Ws11': 4.813,
     'L0_ffn_bs11': 8.0,
     'L0_ffn_Ws2': 4.802,
     'L0_ffn_bs2': 11.93}
    for name, (base, spread) in spreads.items():
        noise = np.random.default_rng([zlib.crc32(name.encode()), seed]).standard_normal(out[name].shape)
        drawn = base * np.exp(spread * noise) if base else spread * noise
        out[name] = jnp.asarray(drawn.astype(out[name].dtype))
    for name, factor in factors.items():
        out[name] = (out[name] * factor).astype(out[name].dtype)
    return out
```

```python
import concourse.bass as bass
from concourse import mybir
from contextlib import ExitStack


def attention_moe_layer(nc, tokens, wq, wk, wv, wo, w_gates, rms_w, Wg, W1, b1, W11, b11, W2, b2,
                        Ws1, bs1, Ws11, bs11, Ws2, bs2, out):
    f32, f32r, bf16 = mybir.dt.float32, mybir.dt.float32r, mybir.dt.bfloat16
    i32, u32 = mybir.dt.int32, mybir.dt.uint32
    ALU, ACT, X = mybir.AluOpType, mybir.ActivationFunctionType, mybir.AxisListType.X

    P = 128
    N, D = tokens.shape[1], tokens.shape[2]
    HEADS, DH = wq.shape[0], wq.shape[2]
    E, H = W1.shape[0], W1.shape[2]
    HS = Ws1.shape[1]
    NT = N // P
    PAIRS = HEADS // 2
    BANK = 512
    BT = BANK // P
    NC = N // BANK
    TOPK = 2
    UP = 2 * H
    HB = H // P
    SB = HS // P
    SLOT_TILES = TOPK * N // P + E
    SLOTS = SLOT_TILES * P
    RMS_EPS = 2.0 ** -23
    LN_EPS = 1e-5
    SCALE = DH ** -0.5
    MASKED = -1e30

    QK_FILLS = 4 * NC
    V_FILLS = NC
    chunks = [[(c, min(BANK, (t + 1) * P - c * BANK)) for c in range(t // BT + 1)] for t in range(NT)]
    S_FILLS = 2 * sum(len(c) for c in chunks)
    FILLS = QK_FILLS + V_FILLS + S_FILLS
    first_fill = {}
    first_group = {}
    f = 0
    for t in range(NT):
        for h in range(2):
            first_fill[t, h] = QK_FILLS + V_FILLS + f
            first_group[t, h] = f
            f += len(chunks[t])
    GROUPS = S_FILLS
    RING = 4

    def group_end(t, h):
        return first_group[t, h] + len(chunks[t])

    ctx = ExitStack()
    with ctx:
        def sb(name, shape, dt, stack=ctx):
            return stack.enter_context(nc.sbuf_tensor(name, shape, dt))

        def sem(name):
            return ctx.enter_context(nc.semaphore(name))

        x_acc = sb("x_acc", [P, NT, D], f32)
        w_up = sb("w_up", [P, E, UP], f32)
        ws_up = sb("ws_up", [P, 2, HS], f32)
        ws_down = sb("ws_down", [P, SB, D], f32)
        wq_sb = sb("wq_sb", [P, HEADS, DH], f32)
        wk_sb = sb("wk_sb", [P, HEADS, DH], f32)
        wv_sb = sb("wv_sb", [P, HEADS * DH], f32)
        wo_sb = sb("wo_sb", [P, PAIRS, D], f32)
        wgate_sb = sb("wgate_sb", [P, HEADS], f32)
        wr_sb = sb("wr_sb", [P, E], f32)
        rmsw = sb("rmsw", [P, 1], f32)
        ident = sb("ident", [P, P], f32)
        zeros = sb("zeros", [P, BANK], f32)
        ident_b = sb("ident_b", [P, P], bf16)
        mask_b = sb("mask_b", [P, P], bf16)
        stat = sb("stat", [P, 4, NT], f32)
        bias_e = sb("bias_e", [E, UP + D], f32)
        bias_r = sb("bias_r", [E, UP + D], f32)
        bias_s = sb("bias_s", [E, 3, UP + D], bf16)
        bias_rows = sb("bias_rows", [3, E * (UP + D)], bf16)
        bs_col = sb("bs_col", [P, 2, SB], f32)
        bs2_all = sb("bs2_all", [P, D], f32)
        ones3 = sb("ones3", [3, P], bf16)
        ones_b = sb("ones_b", [P, P], bf16)
        tri_b = sb("tri_b", [P, P], bf16)
        attn = ExitStack()
        tT = sb("tT", [P, N], f32, attn)
        q_hl = [sb(f"q_hl{h}", [P, N], f32r, attn) for h in range(2)]
        k_h = [sb(f"k_h{h}", [P, N], f32r, attn) for h in range(2)]
        k_l = [sb(f"k_l{h}", [P, N], f32r, attn) for h in range(2)]
        v_sb = sb("v_sb", [P, NT, P], f32, attn)
        probs = [[sb(f"probs{b}{h}", [P, N], f32, attn) for h in range(2)] for b in range(2)]
        xn = probs[0][0][:, :].rearrange("p (n d) -> p n d", d=D)
        probsT = [sb(f"probsT{h}", [P, NT, P], f32, attn) for h in range(2)]
        wqk_d = sb("wqk_d", [P, 4, 2, DH], f32, attn)
        wo_p = sb("wo_p", [P, D], f32, attn)
        outT = [[sb(f"outT{b}{h}", [P, P], f32, attn) for h in range(2)] for b in range(2)]
        gate1 = sb("gate1", [P, NT, HEADS], f32, attn)
        cmax = sb("cmax", [P, 2, NC], f32, attn)
        nmax = sb("nmax", [P, 2 * NT], f32, attn)
        rsum = sb("rsum", [P, 2 * NT], f32, attn)
        rden = sb("rden", [P, 2, 2], f32, attn)
        attn.close()
        moe = ExitStack()
        xT = sb("xT", [P, N], f32, moe)
        w_down = sb("w_down", [P, E, HB, D], f32, moe)
        shared = sb("shared", [P, NT, D], f32, moe)
        logits = sb("logits", [P, NT, E], f32, moe)
        top8 = sb("top8", [P, NT, 8], f32, moe)
        idx8 = sb("idx8", [P, NT, 8], u32, moe)
        idxf = sb("idxf", [P, TOPK, NT], f32, moe)
        ie = sb("ie", [P, NT, E], f32, moe)
        hot = sb("hot", [P, TOPK, NT, E], f32, moe)
        routed = sb("routed", [P, NT * E], bf16, moe)
        rank = sb("rank", [P, NT, E], f32, moe)
        before = sb("before", [P, NT + 1, E], f32, moe)
        cnt_i = sb("cnt_i", [P, E], i32, moe)
        tiles_a = sb("tiles_a", [P, E], f32, moe)
        tiles_b = sb("tiles_b", [P, E], f32, moe)
        tiles_n = sb("tiles_n", [P, E], f32, moe)
        base = sb("base", [P, E], f32, moe)
        picked = sb("picked", [P, TOPK, NT, E], f32, moe)
        slot_f = sb("slot_f", [P, TOPK, NT], f32, moe)
        slot = sb("slot", [P, TOPK, NT], u32, moe)
        it = sb("it", [1, SLOT_TILES, E], f32, moe)
        past = sb("past", [1, SLOT_TILES, E], f32, moe)
        exp_f = sb("exp_f", [1, SLOT_TILES], f32, moe)
        exp_i = sb("exp_i", [1, SLOT_TILES], i32, moe)
        gat = sb("gat", [P, 4, NT], f32, moe)
        bn = sb("bn", [P, NT, 6], f32, moe)
        mv = sb("mv", [P, NT, 2], f32, moe)
        rstd = sb("rstd", [P, 2, NT], f32, moe)
        sil_s = sb("sil_s", [P, 2, BANK], f32, moe)
        act_s = sb("act_s", [P, 2, SB, BANK], f32, moe)
        xg = sb("xg", [P, 2, D], f32, moe)
        xgT = sb("xgT", [P, 2, P], f32, moe)
        sil = sb("sil", [P, 2, H], f32, moe)
        hid = sb("hid", [P, 2, H], f32, moe)
        hidT = sb("hidT", [P, 2, H], f32, moe)
        y_sb = sb("y_sb", [P, 2, D], f32, moe)
        yg = sb("yg", [P, TOPK, NT, D], f32, moe)
        fin = sb("fin", [P, NT, D], f32, moe)
        moe.close()

        x_sorted = nc.dram_tensor("x_sorted", (SLOTS, D), f32, kind="Internal").ap()
        y_sorted = nc.dram_tensor("y_sorted", (SLOTS, D), f32, kind="Internal").ap()

        def bank(name):
            return ctx.enter_context(nc.psum_tensor(name, [P, BANK], f32))

        ps_s = [bank(f"ps_s{i}") for i in range(RING)]
        ps_t = [bank(f"ps_t{i}") for i in range(2)]
        ps_pv = bank("ps_pv")
        ps_wo = bank("ps_wo")

        x_in, w_in, wo_in, gw_in = sem("x_in"), sem("w_in"), sem("wo_in"), sem("gw_in")
        moe_in, shw_in, bias_in, brow_in = sem("moe_in"), sem("shw_in"), sem("bias_in"), sem("brow_in")
        out_done = sem("out_done")
        zero_set, zfill, consts, ident_set = sem("zero_set"), sem("zfill"), sem("consts"), sem("ident_set")
        pool_step = sem("pool_step")
        dve_step, act_step = sem("dve_step"), sem("act_step")
        bias_split = sem("bias_split")
        ms_ready, std_ready, xn_ready, xnT_ready, tT_ready = (sem(n) for n in (
            "ms_ready", "std_ready", "xn_ready", "xnT_ready", "tT_ready"))
        z_ready, ez_ready, gate_ready = sem("z_ready"), sem("ez_ready"), sem("gate_ready")
        pair_w, fill, freed, high = sem("pair_w"), sem("fill"), sem("freed"), sem("high")
        row_max, exp_done = sem("row_max"), sem("exp_done")
        turned, moved0, moved1 = sem("turned"), sem("moved0"), sem("moved1")
        pv_done, out_ready, wo_done, acc_done = sem("pv_done"), sem("out_ready"), sem("wo_done"), sem("acc_done")
        loop_step = sem("loop_step")
        var_ready, ln_std, x1_ready = sem("var_ready"), sem("ln_std"), sem("x1_ready")
        x1T_psum, x1T_ready = sem("x1T_psum"), sem("x1T_ready")
        lg_psum, lg_ready, gexp = sem("lg_psum"), sem("lg_ready"), sem("gexp")
        routed_ready, count_psum, slots_ready, expert_ready = (sem(n) for n in (
            "routed_ready", "count_psum", "slots_ready", "expert_ready"))
        scattered, gathered = sem("scattered"), sem("gathered")
        up_s, sil_done, act_done, down_s, shared_done = (sem(n) for n in (
            "up_s", "sil_done", "act_done", "down_s", "shared_done"))
        xg_in = [sem(f"xg_in{b}") for b in range(2)]
        y_out = [sem(f"y_out{b}") for b in range(2)]
        xgT_psum, xgT_ready, up_e, sil_e, hid_e = (sem(n) for n in (
            "xgT_psum", "xgT_ready", "up_e", "sil_e", "hid_e"))
        hidT_psum, hidT_ready, down_e, y_ready = (sem(n) for n in (
            "hidT_psum", "hidT_ready", "down_e", "y_ready"))
        gate_done, fin_var, fin_std, fin_ready = sem("gate_done"), sem("fin_var"), sem("fin_std"), sem("fin_ready")

        ONE = 1

        block = ctx.enter_context(nc.Block())

        @block.sync
        def _(sp):
            for s in (wo_done, pv_done, turned, freed, moved0, moved1, out_ready, acc_done,
                      xgT_psum, xgT_ready, hid_e, hidT_ready, y_ready):
                sp.sem_inc(s, ONE)
            for s in y_out:
                sp.sem_inc(s, 16 * ONE)
            sp.dma_start(x_acc[:, :, :], tokens[0].rearrange("(n p) d -> p n d", p=P)).then_inc(x_in, 16)
            sp.dma_start(rmsw[:, :], rms_w.rearrange("(p a) -> p a", a=1)).then_inc(gw_in, 16)
            sp.dma_start(wgate_sb[:, :], w_gates).then_inc(gw_in, 16)
            sp.dma_start(wr_sb[:, :], Wg).then_inc(gw_in, 16)
            sp.dma_start(wq_sb[:, :, :], wq.rearrange("h d e -> d h e")).then_inc(w_in, 16)
            sp.dma_start(wk_sb[:, :, :], wk.rearrange("h d e -> d h e")).then_inc(w_in, 16)
            sp.dma_start(wv_sb[:, :].rearrange("d (h e) -> d h e", h=HEADS),
                         wv.rearrange("h d e -> d h e")).then_inc(w_in, 16)
            sp.dma_start(wo_sb[:, :, :], wo.rearrange("(n a) e d -> (a e) n d", a=2)).then_inc(wo_in, 16)
            sp.dma_start(bias_e[:, 0:H], b1).then_inc(bias_in, 16)
            sp.dma_start(bias_e[:, H:UP], b11).then_inc(bias_in, 16)
            sp.dma_start(bias_e[:, UP:], b2).then_inc(bias_in, 16)
            with nc.allow_non_contiguous_dma("a column of biases on each partition, 1 KB"):
                sp.dma_start(bs_col[:, 0, :], bs1.rearrange("(m p) -> p m", p=P)).then_inc(shw_in, 16)
                sp.dma_start(bs_col[:, 1, :], bs11.rearrange("(m p) -> p m", p=P)).then_inc(shw_in, 16)
            sp.dma_start(bs2_all[:, :], bs2.rearrange("(a d) -> a d", a=1).to_broadcast([P, D])).then_inc(shw_in, 16)
            sp.dma_start(ws_up[:, 0, :], Ws1).then_inc(shw_in, 16)
            sp.dma_start(ws_up[:, 1, :], Ws11).then_inc(shw_in, 16)
            sp.dma_start(ws_down[:, :, :], Ws2.rearrange("(m p) d -> p m d", p=P)).then_inc(shw_in, 16)
            sp.dma_start(w_up[:, :, 0:H], W1.rearrange("e d h -> d e h")).then_inc(moe_in, 16)
            sp.dma_start(w_up[:, :, H:], W11.rearrange("e d h -> d e h")).then_inc(moe_in, 16)
            sp.wait_ge(zero_set, 1)
            view = x_sorted.rearrange("(g n p) d -> g p n d", p=P, n=BT)
            for g in range(SLOT_TILES // BT):
                sp.dma_start(view[g], zeros[:, :].rearrange("p (n d) -> p n d", d=D)).then_inc(zfill, 16)
            sp.wait_ge(bias_split, 1)
            for k in range(3):
                sp.dma_start(bias_rows[k:k + 1, :].rearrange("a (e n) -> a e n", e=E),
                             bias_s[:, k, :]).then_inc(brow_in, 16)
            sp.wait_ge(acc_done, ONE + PAIRS * NT)
            sp.dma_start(w_down[:, :, :, :], W2.rearrange("e (m p) d -> p e m d", p=P)).then_inc(moe_in, 16)
            sp.wait_ge(scattered, 16 * TOPK * NT)
            with sp.Fori(0, SLOT_TILES // 2) as i:
                for b in range(2):
                    sp.wait_ge(xgT_psum, ONE + i * 2 + (b - 1 if b else 0))
                    sp.dma_start(xg[:, b, :], x_sorted[bass.ds(i * (2 * P) + b * P, P), :]).then_inc(xg_in[b], 16)
                for b in range(2):
                    sp.wait_ge(y_ready, ONE + i * 2 + b + 1)
                    sp.dma_start(y_sorted[bass.ds(i * (2 * P) + b * P, P), :], y_sb[:, b, :]).then_inc(y_out[b], 16)
            for t in range(NT):
                sp.wait_ge(fin_ready, t + 1)
                sp.dma_start(out[0, t * P:(t + 1) * P, :], fin[:, t, :]).then_inc(out_done, 16)
            sp.wait_ge(out_done, 16 * NT)

        @block.gpsimd
        def _(pool):
            nc.gpsimd.memset(ident[:, :], 0.0).then_inc(pool_step, 1)
            nc.gpsimd.memset(mask_b[:, :], 0.0).then_inc(pool_step, 1)
            nc.gpsimd.memset(tri_b[:, :], 1.0).then_inc(pool_step, 1)
            nc.gpsimd.memset(ones_b[:, :], 1.0).then_inc(consts, 1)
            nc.gpsimd.memset(ones3[:, :], 1.0).then_inc(consts, 1)
            nc.gpsimd.memset(zeros[:, :], 0.0).then_inc(zero_set, 1)
            for b in range(2):
                for h in range(2):
                    nc.gpsimd.memset(outT[b][h][:, :], 0.0).then_inc(consts, 1)
            nc.gpsimd.memset(ident_b[:, :], 0.0).then_inc(pool_step, 1)
            pool.wait_ge(pool_step, 4)
            nc.gpsimd.affine_select(out=ident[:, :], in_=ident[:, :], compare_op=ALU.not_equal, fill=1.0,
                                    base=0, pattern=[[-1, P]], channel_multiplier=1).then_inc(ident_set, 1)
            nc.gpsimd.affine_select(out=ident_b[:, :], in_=ident_b[:, :], compare_op=ALU.not_equal, fill=1.0,
                                    base=0, pattern=[[-1, P]], channel_multiplier=1).then_inc(ident_set, 1)
            nc.gpsimd.affine_select(out=mask_b[:, :], in_=mask_b[:, :], compare_op=ALU.is_ge,
                                    fill=MASKED, base=0, pattern=[[-1, P]], channel_multiplier=1).then_inc(consts, 1)
            nc.gpsimd.affine_select(out=tri_b[:, :], in_=tri_b[:, :], compare_op=ALU.is_gt, fill=0.0,
                                    base=0, pattern=[[1, P]], channel_multiplier=-1).then_inc(consts, 1)
            pool.wait_ge(w_in, 48)
            pool.wait_ge(wo_in, 16)
            with pool.Fori(0, PAIRS) as p:
                pool.wait_ge(wo_done, ONE + p * NT)
                for n, w in enumerate((wq_sb, wk_sb)):
                    nc.gpsimd.tensor_copy(wqk_d[:, 2 * n:2 * n + 2, 0, :],
                                          w[:, bass.ds(p * 2, 2), :]).then_inc(pair_w, 1)
                    nc.gpsimd.tensor_copy(wqk_d[:, 2 * n:2 * n + 2, 1, :],
                                          w[:, bass.ds(p * 2, 2), :]).then_inc(pair_w, 1)
                nc.gpsimd.tensor_copy(wo_p[:, :], wo_sb[:, bass.ds(p, 1), :]
                                      .rearrange("d a e -> d (a e)")).then_inc(pair_w, 1)
            pool.wait_ge(acc_done, ONE + PAIRS * NT)
            nc.gpsimd.iota(ie[:, :, :], pattern=[[0, NT], [1, E]], base=0, channel_multiplier=0,
                           allow_small_or_imprecise_dtypes=True).then_inc(pool_step, 1)
            nc.gpsimd.iota(it[:, :, :], pattern=[[1, SLOT_TILES], [0, E]], base=0, channel_multiplier=0,
                           allow_small_or_imprecise_dtypes=True).then_inc(pool_step, 1)
            pool.wait_ge(zfill, 16 * (SLOT_TILES // BT))
            pool.wait_ge(slots_ready, 1)
            for t in range(NT):
                for k in range(TOPK):
                    nc.gpsimd.indirect_dma_start(
                        out=x_sorted, out_offset=bass.IndirectOffsetOnAxis(ap=slot[:, k, t:t + 1], axis=0),
                        in_=x_acc[:, t, :], in_offset=None).then_inc(scattered, 16)
            for b in range(2):
                pool.wait_ge(y_out[b], 16 * ONE + 16 * (SLOT_TILES // 2))
            for t in range(NT):
                for k in range(TOPK):
                    nc.gpsimd.indirect_dma_start(
                        out=yg[:, k, t, :], out_offset=None, in_=y_sorted,
                        in_offset=bass.IndirectOffsetOnAxis(ap=slot[:, k, t:t + 1], axis=0)).then_inc(gathered, 16)
            pool.wait_ge(gathered, 16 * TOPK * NT)
            nc.gpsimd.memset(zeros[:, 0:1], 0.0).then_inc(gate_done, 1)

        @block.scalar
        def _(act):
            act.wait_ge(ms_ready, 1)
            nc.scalar.activation(stat[:, 1, :], stat[:, 0, :], ACT.Sqrt).then_inc(std_ready, 1)
            act.wait_ge(z_ready, 1)
            nc.scalar.activation(gate1[:, :, :].rearrange("p n h -> p (n h)"), ps_t[0][:, 0:NT * HEADS], ACT.Exp,
                                 scale=-1.0).then_inc(ez_ready, 1)

            with act.Fori(0, PAIRS) as p:
                for n in range(QK_FILLS):
                    w, c = n // NC, n % NC
                    act.wait_ge(fill, p * FILLS + (n + 1))
                    dst = q_hl[w] if w < 2 else k_h[w - 2]
                    nc.scalar.activation(dst[:, c * BANK:(c + 1) * BANK], ps_s[n % RING][:, :],
                                         ACT.Copy).then_inc(high, 1)

                def exps(t):
                    for h in range(2):
                        act.wait_ge(row_max, p * (2 * NT) + (2 * t + h + 1))
                        w = (t + 1) * P
                        nc.scalar.activation(probs[t % 2][h][:, 0:w], probs[t % 2][h][:, 0:w], ACT.Exp,
                                             bias=nmax[:, 2 * t + h:2 * t + h + 1], scale=SCALE,
                                             accum_out=rsum[:, 2 * t + h:2 * t + h + 1]).then_inc(exp_done, 1)

                def move(t):
                    act.wait_ge(pv_done, ONE + p * NT + t)
                    for h in range(2):
                        for c, w in chunks[t]:
                            g = first_group[t, h] + c
                            if g % 2 == 0:
                                act.wait_ge(turned, ONE + p * GROUPS + (g + 1))
                                nc.scalar.activation(
                                    probsT[h][:, c * BT:c * BT + w // P, :].rearrange("p n i -> p (n i)"),
                                    ps_t[0][:, 0:w], ACT.Copy).then_inc(moved0, 1)

                def unload(t):
                    act.wait_ge(pv_done, ONE + p * NT + (t + 1))
                    act.wait_ge(wo_done, ONE + p * NT + max(t - 1, 0))
                    for h in range(2):
                        rows = slice(h * DH, (h + 1) * DH)
                        nc.scalar.activation(outT[t % 2][h][rows, :], ps_pv[rows, 0:P], ACT.Copy).then_inc(out_ready, 1)

                for s in range(NT + 2):
                    if s < NT:
                        exps(s)
                    if s >= 2:
                        unload(s - 2)
                    if 1 <= s <= NT:
                        move(s - 1)

            act.wait_ge(var_ready, 1)
            nc.scalar.activation(rstd[:, 0, :], rstd[:, 1, :], ACT.Sqrt).then_inc(ln_std, 1)
            act.wait_ge(gexp, 1)
            nc.scalar.activation(gat[:, 1, :], gat[:, 0, :], ACT.Exp).then_inc(gexp, 1)
            act.wait_ge(shw_in, 16 * 6)
            for c in range(NC):
                for m in range(SB):
                    n = c * SB + m
                    act.wait_ge(up_s, n + 1)
                    if n >= 2:
                        act.wait_ge(act_done, n - 1)
                    nc.scalar.activation(sil_s[:, n % 2, :], ps_s[2 * (n % 2)][:, :], ACT.Silu,
                                         bias=bs_col[:, 0, m:m + 1]).then_inc(sil_done, 1)
            with act.Fori(0, SLOT_TILES // 2) as i:
                for b in range(2):
                    act.wait_ge(xgT_psum, ONE + i * 2 + (b + 1))
                    nc.scalar.activation(xgT[:, b, :], ps_t[b][:, 0:P], ACT.Copy).then_inc(xgT_ready, 1)
                    act.wait_ge(up_e, i * 2 + (b + 1))
                    nc.scalar.activation(sil[:, b, :], ps_s[b][:, 0:H], ACT.Silu).then_inc(sil_e, 1)
                    act.wait_ge(down_e, i * 2 + (b + 1))
                    act.wait_ge(y_out[b], 16 * ONE + i * 16)
                    nc.scalar.activation(y_sb[:, b, :], (ps_pv, ps_wo)[b][:, 0:D], ACT.Copy).then_inc(y_ready, 1)
            act.wait_ge(fin_var, 1)
            nc.scalar.activation(rstd[:, 0, :], rstd[:, 1, :], ACT.Sqrt).then_inc(fin_std, 1)

        @block.vector
        def _(dve):
            steps = [0]

            def link(ins):
                steps[0] += 1
                ins.then_inc(dve_step, 1)
                dve.wait_ge(dve_step, steps[0])

            dve.wait_ge(x_in, 16)
            for t in range(NT):
                ins = nc.vector.tensor_tensor_reduce(out=xn[:, t, :], in0=x_acc[:, t, :], in1=x_acc[:, t, :],
                                                     scale=1.0 / D, scalar=RMS_EPS, op0=ALU.mult, op1=ALU.add,
                                                     accum_out=stat[:, 0, t:t + 1])
            ins.then_inc(ms_ready, 1)
            dve.wait_ge(bias_in, 48)
            link(nc.vector.tensor_copy(bias_s[:, 0, :], bias_e[:, :]))
            link(nc.vector.tensor_tensor(bias_r[:, :], bias_e[:, :], bias_s[:, 0, :], ALU.subtract))
            link(nc.vector.tensor_copy(bias_s[:, 1, :], bias_r[:, :]))
            link(nc.vector.tensor_tensor(bias_e[:, :], bias_r[:, :], bias_s[:, 1, :], ALU.subtract))
            nc.vector.tensor_copy(bias_s[:, 2, :], bias_e[:, :]).then_inc(bias_split, 1)
            dve.wait_ge(std_ready, 1)
            link(nc.vector.reciprocal(stat[:, 2, :], stat[:, 1, :]))
            for t in range(NT):
                nc.vector.tensor_scalar(xn[:, t, :], x_acc[:, t, :], stat[:, 2, t:t + 1], None,
                                        ALU.mult).then_inc(xn_ready, 1)
            dve.wait_ge(gw_in, 48)
            for c in range(NC):
                dve.wait_ge(xnT_ready, c + 1)
                nc.vector.tensor_scalar(tT[:, c * BANK:(c + 1) * BANK], ps_s[c][:, :], rmsw[:, 0:1], None,
                                        ALU.mult).then_inc(tT_ready, 1)
            dve.wait_ge(ez_ready, 1)
            nc.vector.tensor_scalar(gate1[:, :, :], gate1[:, :, :], 1.0, None, ALU.add).then_inc(gate_ready, 1)
            dve.wait_ge(gate_ready, 1)
            dve.wait_ge(consts, 8)

            LINKS = 5 * NT
            with dve.Fori(0, PAIRS) as p:
                count = [0]

                def link_in(ins):
                    count[0] += 1
                    ins.then_inc(loop_step, 1)
                    dve.wait_ge(loop_step, p * LINKS + count[0])

                for n in range(QK_FILLS):
                    w, c = n // NC, n % NC
                    cols = slice(c * BANK, (c + 1) * BANK)
                    dve.wait_ge(high, p * QK_FILLS + (n + 1))
                    if w < 2:
                        nc.vector.tensor_tensor(q_hl[w][DH:, cols], ps_s[n % RING][DH:, :],
                                                q_hl[w][DH:, cols].bitcast(f32), ALU.subtract).then_inc(freed, 1)
                    else:
                        nc.vector.tensor_tensor(k_l[w - 2][:, cols], ps_s[n % RING][:, :],
                                                k_h[w - 2][:, cols].bitcast(f32), ALU.subtract).then_inc(freed, 1)
                for c in range(V_FILLS):
                    n = QK_FILLS + c
                    dve.wait_ge(fill, p * FILLS + (n + 1))
                    nc.vector.tensor_copy(v_sb[:, c * BT:(c + 1) * BT, :].rearrange("p n e -> p (n e)"),
                                          ps_s[n % RING][:, :]).then_inc(freed, 1)

                def scores(t):
                    for h in range(2):
                        dve.wait_ge(turned, ONE + p * GROUPS + (group_end(t - 2, h) if t >= 2 else 0))
                        for c, w in chunks[t]:
                            n = first_fill[t, h] + c
                            dve.wait_ge(fill, p * FILLS + (n + 1))
                            ins = nc.vector.tensor_scalar(
                                probs[t % 2][h][:, c * BANK:c * BANK + w], ps_s[n % RING][:, 0:w], 1.0, None,
                                ALU.mult, ALU.max, accum_out=cmax[:, h, c:c + 1])
                            ins.then_inc(freed, 1)
                        dve.wait_ge(freed, ONE + p * FILLS + (n + 1))
                        link_in(nc.vector.tensor_reduce(nmax[:, 2 * t + h:2 * t + h + 1],
                                                        cmax[:, h, 0:len(chunks[t])], X, ALU.max, negate=True))
                        nc.vector.tensor_scalar(nmax[:, 2 * t + h:2 * t + h + 1], nmax[:, 2 * t + h:2 * t + h + 1],
                                                SCALE, None, ALU.mult).then_inc(row_max, 1)

                def move(t):
                    dve.wait_ge(pv_done, ONE + p * NT + t)
                    for h in range(2):
                        for c, w in chunks[t]:
                            g = first_group[t, h] + c
                            if g % 2 == 1:
                                dve.wait_ge(turned, ONE + p * GROUPS + (g + 1))
                                nc.vector.tensor_copy(
                                    probsT[h][:, c * BT:c * BT + w // P, :].rearrange("p n i -> p (n i)"),
                                    ps_t[1][:, 0:w]).then_inc(moved1, 1)

                def add(t):
                    dve.wait_ge(exp_done, p * (2 * NT) + (2 * t + 2))
                    r = rden[:, t % 2, :]
                    link_in(nc.vector.tensor_tensor(r, rsum[:, 2 * t:2 * t + 2],
                                                    gate1[:, t, bass.ds(p * 2, 2)], ALU.mult))
                    link_in(nc.vector.reciprocal(r, r))
                    dve.wait_ge(wo_done, ONE + p * NT + (t + 1))
                    link_in(nc.vector.scalar_tensor_tensor(
                        out=x_acc[:, t, :], in0=ps_wo[:, 0:D], scalar=rden[:, t % 2, 0:1], in1=x_acc[:, t, :],
                        op0=ALU.mult, op1=ALU.add))
                    nc.vector.scalar_tensor_tensor(
                        out=x_acc[:, t, :], in0=ps_wo[:, D:2 * D], scalar=rden[:, t % 2, 1:2], in1=x_acc[:, t, :],
                        op0=ALU.mult, op1=ALU.add).then_inc(acc_done, 1)

                for s in range(NT + 3):
                    if s < NT:
                        scores(s)
                    if 1 <= s <= NT:
                        move(s - 1)
                    if s >= 3:
                        add(s - 3)
                assert count[0] == LINKS

            def layer_norm(src, ready_sem, std_sem):
                for t in range(NT):
                    ins = nc.vector.bn_stats(bn[:, t, :], src(t))
                link(ins)
                for t in range(NT):
                    ins = nc.vector.bn_aggr(mv[:, t, :], bn[:, t, :])
                link(ins)
                nc.vector.tensor_scalar(rstd[:, 1, :], mv[:, :, 1], LN_EPS, None, ALU.add).then_inc(ready_sem, 1)
                dve.wait_ge(std_sem, 1)
                link(nc.vector.reciprocal(rstd[:, 1, :], rstd[:, 0, :]))

            dve.wait_ge(acc_done, ONE + PAIRS * NT)
            layer_norm(lambda t: x_acc[:, t, :], var_ready, ln_std)
            for t in range(NT):
                nc.vector.tensor_scalar(x_acc[:, t, :], x_acc[:, t, :], mv[:, t, 0:1], rstd[:, 1, t:t + 1],
                                        ALU.subtract, ALU.mult).then_inc(x1_ready, 1)
            for c in range(NC):
                dve.wait_ge(x1T_psum, c + 1)
                nc.vector.tensor_copy(xT[:, c * BANK:(c + 1) * BANK], ps_s[c][:, :]).then_inc(x1T_ready, 1)
            dve.wait_ge(lg_psum, 1)
            link(nc.vector.tensor_copy(logits[:, :, :].rearrange("p n e -> p (n e)"), ps_t[0][:, 0:NT * E]))
            for t in range(NT):
                ins = nc.vector.max(top8[:, t, :], logits[:, t, :])
            link(ins)
            for t in range(NT):
                ins = nc.vector.max_index(idx8[:, t, :], top8[:, t, :], logits[:, t, :])
            link(ins)
            for k in range(TOPK):
                ins = nc.vector.tensor_copy(idxf[:, k, :], idx8[:, :, k])
            link(ins)
            dve.wait_ge(pool_step, 6)
            for k in range(TOPK):
                ins = nc.vector.tensor_tensor(hot[:, k], ie[:, :, :],
                                              idxf[:, k, :].unsqueeze(2).to_broadcast([P, NT, E]), ALU.is_equal)
            link(ins)
            nc.vector.tensor_tensor(routed[:, :].rearrange("p (n e) -> p n e", e=E), hot[:, 0], hot[:, 1],
                                    ALU.add).then_inc(routed_ready, 1)
            nc.vector.tensor_tensor(gat[:, 0, :], top8[:, :, 1], top8[:, :, 0], ALU.subtract).then_inc(gexp, 1)
            dve.wait_ge(count_psum, 1)
            link(nc.vector.tensor_copy(rank[:, :, :].rearrange("p n e -> p (n e)"), ps_t[1][:, 0:NT * E]))
            link(nc.vector.memset(before[:, 0, :], 0.0))
            for t in range(NT):
                link(nc.vector.tensor_tensor(before[:, t + 1, :], before[:, t, :],
                                             ps_pv[:, t * E:(t + 1) * E], ALU.add))
            link(nc.vector.tensor_scalar(tiles_a[:, :], before[:, NT, :], float(P - 1), None, ALU.add))
            link(nc.vector.tensor_copy(cnt_i[:, :], tiles_a[:, :]))
            link(nc.vector.tensor_scalar(cnt_i[:, :], cnt_i[:, :], P.bit_length() - 1, None,
                                         ALU.logical_shift_right))
            link(nc.vector.tensor_copy(tiles_n[:, :], cnt_i[:, :]))
            link(nc.vector.tensor_copy(tiles_a[:, :], tiles_n[:, :]))
            src, dst, d = tiles_a, tiles_b, 1
            while d < E:
                link(nc.vector.tensor_copy(dst[:, 0:d], src[:, 0:d]))
                link(nc.vector.tensor_tensor(dst[:, d:], src[:, d:], src[:, 0:E - d], ALU.add))
                src, dst, d = dst, src, 2 * d
            link(nc.vector.tensor_tensor(base[:, :], src[:, :], tiles_n[:, :], ALU.subtract))
            link(nc.vector.tensor_scalar(base[:, :], base[:, :], float(P), None, ALU.mult))
            link(nc.vector.tensor_tensor(rank[:, :, :], rank[:, :, :], before[:, 0:NT, :], ALU.add))
            link(nc.vector.tensor_tensor(rank[:, :, :], rank[:, :, :],
                                         base[:, :].unsqueeze(1).to_broadcast([P, NT, E]), ALU.add))
            for k in range(TOPK):
                link(nc.vector.tensor_tensor(picked[:, k], hot[:, k], rank[:, :, :], ALU.mult))
                link(nc.vector.tensor_reduce(slot_f[:, k, :], picked[:, k], X, ALU.add))
            nc.vector.tensor_copy(slot[:, :, :], slot_f[:, :, :]).then_inc(slots_ready, 1)
            link(nc.vector.tensor_tensor(past[:, :, :], it[:, :, :],
                                         src[0:1, :].unsqueeze(1).to_broadcast([1, SLOT_TILES, E]), ALU.is_ge))
            link(nc.vector.tensor_reduce(exp_f[:, :], past[:, :, :], X, ALU.add))
            link(nc.vector.tensor_scalar(exp_f[:, :], exp_f[:, :], float(E - 1), None, ALU.min))
            nc.vector.tensor_copy(exp_i[:, :], exp_f[:, :]).then_inc(expert_ready, 1)
            dve.wait_ge(gexp, 2)
            link(nc.vector.tensor_scalar(gat[:, 2, :], gat[:, 1, :], 1.0, None, ALU.add))
            link(nc.vector.reciprocal(gat[:, 2, :], gat[:, 2, :]))
            link(nc.vector.tensor_tensor(gat[:, 3, :], gat[:, 1, :], gat[:, 2, :], ALU.mult))
            dve.wait_ge(shw_in, 16 * 6)
            for t in range(NT):
                ins = nc.vector.tensor_tensor(shared[:, t, :], x_acc[:, t, :], bs2_all[:, :], ALU.add)
            link(ins)

            def shared_add(c):
                dve.wait_ge(down_s, c + 1)
                sh = shared[:, c * BT:(c + 1) * BT, :].rearrange("p n d -> p (n d)")
                nc.vector.tensor_tensor(sh, ps_t[c % 2][:, :], sh, ALU.add).then_inc(shared_done, 1)

            for c in range(NC):
                for m in range(SB):
                    n = c * SB + m
                    dve.wait_ge(sil_done, n + 1)
                    if c >= 2 and m == 0:
                        dve.wait_ge(down_s, c - 1)
                    nc.vector.scalar_tensor_tensor(out=act_s[:, c % 2, m, :], in0=ps_s[2 * (n % 2) + 1][:, :],
                                                   scalar=bs_col[:, 1, m:m + 1], in1=sil_s[:, n % 2, :],
                                                   op0=ALU.add, op1=ALU.mult).then_inc(act_done, 1)
                if c >= 1:
                    shared_add(c - 1)
            shared_add(NC - 1)
            with dve.Fori(0, SLOT_TILES // 2) as i:
                for b in range(2):
                    dve.wait_ge(sil_e, i * 2 + (b + 1))
                    nc.vector.tensor_tensor(hid[:, b, :], ps_s[b][:, H:UP], sil[:, b, :], ALU.mult).then_inc(hid_e, 1)
                    dve.wait_ge(hidT_psum, i * 2 + (b + 1))
                    nc.vector.tensor_copy(hidT[:, b, :], ps_s[2 + b][:, 0:H]).then_inc(hidT_ready, 1)
            dve.wait_ge(gate_done, 1)
            dve.wait_ge(shared_done, NC)
            for k in range(TOPK):
                for t in range(NT):
                    ins = nc.vector.scalar_tensor_tensor(out=shared[:, t, :], in0=yg[:, k, t, :],
                                                         scalar=gat[:, 2 + k, t:t + 1], in1=shared[:, t, :],
                                                         op0=ALU.mult, op1=ALU.add)
                link(ins)
            layer_norm(lambda t: shared[:, t, :], fin_var, fin_std)
            for t in range(NT):
                nc.vector.tensor_scalar(fin[:, t, :], shared[:, t, :], mv[:, t, 0:1], rstd[:, 1, t:t + 1],
                                        ALU.subtract, ALU.mult).then_inc(fin_ready, 1)

        @block.tensor
        def _(pe):
            def turn(dst, src):
                return nc.tensor.transpose(dst, src, ident[:, :])

            pe.wait_ge(ident_set, 1)
            for c in range(NC):
                pe.wait_ge(xn_ready, BT * (c + 1))
                for j in range(BT):
                    mm = turn(ps_s[c][:, j * P:(j + 1) * P], xn[:, c * BT + j, :])
                mm.then_inc(xnT_ready, 1)
            pe.wait_ge(gw_in, 48)
            pe.wait_ge(tT_ready, NC)
            for t in range(NT):
                mm = nc.tensor.matmul(ps_t[0][:, t * HEADS:(t + 1) * HEADS], tT[:, t * P:(t + 1) * P],
                                      wgate_sb[:, :], start=True, stop=True)
            mm.then_inc(z_ready, 1)
            pe.wait_ge(w_in, 48)
            pe.wait_ge(consts, 8)
            pe.wait_ge(ident_set, 2)
            pe.wait_ge(ez_ready, 1)

            with pe.Fori(0, PAIRS) as p:
                pe.wait_ge(pair_w, p * 5 + 5)

                def free_bank(n):
                    pe.wait_ge(freed, ONE + p * FILLS + max(n - RING + 1, 0))

                for n in range(QK_FILLS):
                    w, c = n // NC, n % NC
                    free_bank(n)
                    nc.tensor.matmul(ps_s[n % RING][:, :], wqk_d[:, w].rearrange("d a e -> d (a e)"),
                                     tT[:, c * BANK:(c + 1) * BANK], start=True, stop=True).then_inc(fill, 1)
                for c in range(V_FILLS):
                    n = QK_FILLS + c
                    free_bank(n)
                    for j in range(BT):
                        t = c * BT + j
                        mm = nc.tensor.matmul(ps_s[n % RING][:, j * P:(j + 1) * P], tT[:, t * P:(t + 1) * P],
                                              wv_sb[:, bass.ds(p * P, P)], start=True, stop=True)
                    mm.then_inc(fill, 1)
                pe.wait_ge(freed, ONE + p * FILLS + (QK_FILLS + V_FILLS))

                def scores(t):
                    for h in range(2):
                        for c, w in chunks[t]:
                            n = first_fill[t, h] + c
                            free_bank(n)
                            q = q_hl[h][:, t * P:(t + 1) * P]
                            nc.tensor.matmul(ps_s[n % RING][:, 0:w], q, k_h[h][:, c * BANK:c * BANK + w],
                                             start=True, stop=False)
                            if c == len(chunks[t]) - 1:
                                nc.tensor.matmul(ps_s[n % RING][:, w - P:w], ident_b[:, :], mask_b[:, :],
                                                 start=False, stop=False, skip_group_check=True)
                            nc.tensor.matmul(ps_s[n % RING][:, 0:w], q, k_l[h][:, c * BANK:c * BANK + w],
                                             start=False, stop=True).then_inc(fill, 1)

                def turn_probs(t):
                    for h in range(2):
                        pe.wait_ge(exp_done, p * (2 * NT) + (2 * t + h + 1))
                        for c, w in chunks[t]:
                            g = first_group[t, h] + c
                            pe.wait_ge((moved0, moved1)[g % 2], ONE + p * (GROUPS // 2) + g // 2)
                            for j in range(w // P):
                                at = c * BANK + j * P
                                mm = turn(ps_t[g % 2][:, j * P:(j + 1) * P], probs[t % 2][h][:, at:at + P])
                            mm.then_inc(turned, 1)

                def times_v(t):
                    done = group_end(t, 1)
                    pe.wait_ge(moved0, ONE + p * (GROUPS // 2) + (done + 1) // 2)
                    pe.wait_ge(moved1, ONE + p * (GROUPS // 2) + done // 2)
                    pe.wait_ge(out_ready, ONE + p * (2 * NT) + 2 * t)
                    for j in range(t + 1):
                        for h in range(2):
                            rows = slice(h * DH, (h + 1) * DH)
                            mm = nc.tensor.matmul(ps_pv[rows, 0:P], v_sb[:, j, rows], probsT[h][:, j, :],
                                                  start=(j == 0), stop=(j == t))
                    mm.then_inc(pv_done, 1)

                def times_wo(t):
                    pe.wait_ge(out_ready, ONE + p * (2 * NT) + (2 * t + 2))
                    pe.wait_ge(acc_done, ONE + p * NT + t)
                    for h in range(2):
                        mm = nc.tensor.matmul(ps_wo[:, h * D:(h + 1) * D], outT[t % 2][h][:, :], wo_p[:, :],
                                              start=True, stop=True)
                    mm.then_inc(wo_done, 1)

                for s in range(NT + 3):
                    if s < NT:
                        scores(s)
                    if 2 <= s < NT + 2:
                        times_v(s - 2)
                    if 1 <= s <= NT:
                        turn_probs(s - 1)
                    if s >= 3:
                        times_wo(s - 3)

            for c in range(NC):
                pe.wait_ge(x1_ready, BT * (c + 1))
                for j in range(BT):
                    mm = turn(ps_s[c][:, j * P:(j + 1) * P], x_acc[:, c * BT + j, :])
                mm.then_inc(x1T_psum, 1)
            pe.wait_ge(x1T_ready, NC)
            for t in range(NT):
                mm = nc.tensor.matmul(ps_t[0][:, t * E:(t + 1) * E], xT[:, t * P:(t + 1) * P], wr_sb[:, :],
                                      start=True, stop=True)
            mm.then_inc(lg_psum, 1)
            pe.wait_ge(routed_ready, 1)
            nc.tensor.matmul(ps_t[1][:, 0:NT * E], tri_b[:, :], routed[:, :], start=True, stop=True)
            nc.tensor.matmul(ps_pv[:, 0:NT * E], ones_b[:, :], routed[:, :], start=True, stop=True).then_inc(count_psum, 1)
            pe.wait_ge(shw_in, 16 * 6)

            def shared_down(c):
                pe.wait_ge(act_done, SB * (c + 1))
                if c >= 2:
                    pe.wait_ge(shared_done, c - 1)
                for j in range(BT):
                    for m in range(SB):
                        mm = nc.tensor.matmul(ps_t[c % 2][:, j * P:(j + 1) * P],
                                              act_s[:, c % 2, m, j * P:(j + 1) * P], ws_down[:, m, :],
                                              start=(m == 0), stop=(m == SB - 1))
                mm.then_inc(down_s, 1)

            pe.wait_ge(slots_ready, 1)
            for c in range(NC):
                for m in range(SB):
                    n = c * SB + m
                    if n >= 2:
                        pe.wait_ge(act_done, n - 1)
                    for a in range(2):
                        mm = nc.tensor.matmul(ps_s[2 * (n % 2) + a][:, :], ws_up[:, a, m * P:(m + 1) * P],
                                              xT[:, c * BANK:(c + 1) * BANK], start=True, stop=True)
                    mm.then_inc(up_s, 1)
                if c >= 1:
                    shared_down(c - 1)
            shared_down(NC - 1)
            pe.wait_ge(moe_in, 48)
            pe.wait_ge(brow_in, 48)
            pe.wait_ge(expert_ready, 1)
            pe.wait_ge(shared_done, NC)
            with pe.Fori(0, SLOT_TILES // 2) as i:
                for b in range(2):
                    e = pe.value_load(exp_i[0:1, bass.ds(i * 2 + b, 1)], min_val=0, max_val=E - 1)
                    pe.wait_ge(xg_in[b], i * 16 + 16)
                    pe.wait_ge(xgT_ready, ONE + i * 2 + b)
                    turn(ps_t[b][:, 0:P], xg[:, b, :]).then_inc(xgT_psum, 1)
                    pe.wait_ge(xgT_ready, ONE + i * 2 + (b + 1))
                    pe.wait_ge(hid_e, ONE + i * 2 + b)
                    nc.tensor.matmul(ps_s[b][:, :], ones3[:, :], bias_rows[:, bass.ds(e * (UP + D), UP)],
                                     start=True, stop=False)
                    nc.tensor.matmul(ps_s[b][:, :], xgT[:, b, :],
                                     w_up[:, bass.ds(e, 1), :].rearrange("p a n -> p (a n)"),
                                     start=False, stop=True).then_inc(up_e, 1)
                    pe.wait_ge(hid_e, ONE + i * 2 + (b + 1))
                    pe.wait_ge(hidT_ready, ONE + i * 2 + b)
                    for m in range(HB):
                        mm = turn(ps_s[2 + b][:, m * P:(m + 1) * P], hid[:, b, m * P:(m + 1) * P])
                    mm.then_inc(hidT_psum, 1)
                    pe.wait_ge(hidT_ready, ONE + i * 2 + (b + 1))
                    pe.wait_ge(y_ready, ONE + i * 2 + b)
                    y = (ps_pv, ps_wo)[b][:, 0:D]
                    nc.tensor.matmul(y, ones3[:, :], bias_rows[:, bass.ds(e * (UP + D) + UP, D)],
                                     start=True, stop=False)
                    for m in range(HB):
                        mm = nc.tensor.matmul(y, hidT[:, b, m * P:(m + 1) * P],
                                              w_down[:, bass.ds(e, 1), m, :].rearrange("p a n -> p (a n)"),
                                              start=False, stop=(m == HB - 1))
                    mm.then_inc(down_e, 1)


_INS = ['L0_attn_tokens', 'L0_attn_wq', 'L0_attn_wk', 'L0_attn_wv', 'L0_attn_wo', 'L0_attn_w_gates', 'L0_attn_rms_w',
        'L0_ffn_Wg', 'L0_ffn_W1', 'L0_ffn_b1', 'L0_ffn_W11', 'L0_ffn_b11', 'L0_ffn_W2', 'L0_ffn_b2',
        'L0_ffn_Ws1', 'L0_ffn_bs1', 'L0_ffn_Ws11', 'L0_ffn_bs11', 'L0_ffn_Ws2', 'L0_ffn_bs2']


def kernel(**inputs):
    import numpy as _np
    import concourse.bacc as _bacc
    from concourse import mybir as _mybir
    from concourse.bass_utils import run_bass_kernel_spmd as _run

    nc = _bacc.Bacc("TRN2", target_bir_lowering=False, num_devices=1)
    arrays, aps = {}, {}
    for name in _INS:
        a = _np.ascontiguousarray(inputs[name])
        arrays[f"in_{name}"] = a
        short = name.replace("L0_attn_", "").replace("L0_ffn_", "")
        aps[short] = nc.dram_tensor(f"in_{name}", a.shape, _mybir.dt.from_np(a.dtype), kind="ExternalInput").ap()
    aps["out"] = nc.dram_tensor("out_0", (1, 2048, 128), _mybir.dt.float32, kind="ExternalOutput").ap()
    attention_moe_layer(nc, **aps)
    r = _run(nc, [arrays], core_ids=[0])
    return r.results[0]["out_0"]
```

```python
import concourse.bass as bass
from concourse import mybir
from contextlib import ExitStack


def attention_moe_layer(nc, tokens, wq, wk, wv, wo, w_gates, rms_w, Wg, W1, b1, W11, b11, W2, b2,
                        Ws1, bs1, Ws11, bs11, Ws2, bs2, out):
    f32, f32r, bf16 = mybir.dt.float32, mybir.dt.float32r, mybir.dt.bfloat16
    i32, u32 = mybir.dt.int32, mybir.dt.uint32
    ALU, ACT, X = mybir.AluOpType, mybir.ActivationFunctionType, mybir.AxisListType.X

    P = 128
    N, D = tokens.shape[1], tokens.shape[2]
    HEADS, DH = wq.shape[0], wq.shape[2]
    E, H = W1.shape[0], W1.shape[2]
    HS = Ws1.shape[1]
    NT = N // P
    PAIRS = HEADS // 2
    BANK = 512
    BT = BANK // P
    NC = N // BANK
    TOPK = 2
    UP = 2 * H
    HB = H // P
    SB = HS // P
    SLOT_TILES = TOPK * N // P + E
    SLOTS = SLOT_TILES * P
    RMS_EPS = 2.0 ** -23
    LN_EPS = 1e-5
    SCALE = DH ** -0.5
    MASKED = -1e30

    ORDER = list(range(1, NT, 2)) + list(reversed(range(0, NT, 2)))
    chunks = [[(c, min(BANK, (t + 1) * P - c * BANK)) for c in range(t // BT + 1)] for t in ORDER]
    QK_FILLS = 4 * NC
    V_FILLS = NC
    GROUPS = 2 * sum(len(c) for c in chunks)
    FILLS = QK_FILLS + V_FILLS + GROUPS
    RING = 4
    first = {}
    for s in range(NT):
        for h in range(2):
            first[s, h] = 2 * sum(len(c) for c in chunks[:s]) + h * len(chunks[s])

    def first_fill(s, h):
        return QK_FILLS + V_FILLS + first[s, h]

    def group_end(s, h):
        return first[s, h] + len(chunks[s])

    def step_units(s):
        units = []
        if s < NT:
            units += [("scores", s, h, c, w) for h in range(2) for c, w in chunks[s]]
        stages = [units]
        if 1 <= s <= NT:
            stages.append([("turn", s - 1, h, c, w) for h in range(2) for c, w in chunks[s - 1]])
        if 2 <= s < NT + 2:
            stages.append([("times_v", s - 2, 0, c, w) for c, w in chunks[s - 2]])
        if s >= 3:
            stages.append([("times_wo", s - 3, 0, 0, 0)])
        placed = [((i + 0.5) / len(u), k, x) for k, u in enumerate(stages) for i, x in enumerate(u)]
        return [x for _, _, x in sorted(placed, key=lambda y: y[:2])]

    STEPS = [step_units(s) for s in range(NT + 3)]

    ctx = ExitStack()
    with ctx:
        def sb(name, shape, dt, stack=ctx):
            return stack.enter_context(nc.sbuf_tensor(name, shape, dt))

        def sem(name):
            return ctx.enter_context(nc.semaphore(name))

        x_acc = sb("x_acc", [P, NT, D], f32)
        ws_up = sb("ws_up", [P, 2, HS], f32)
        ws_down = sb("ws_down", [P, SB, D], f32)
        wq_sb = sb("wq_sb", [P, HEADS, DH], f32)
        wk_sb = sb("wk_sb", [P, HEADS, DH], f32)
        wv_sb = sb("wv_sb", [P, HEADS * DH], f32)
        wo_sb = sb("wo_sb", [P, PAIRS, D], f32)
        wgate_sb = sb("wgate_sb", [P, HEADS], f32)
        wr_sb = sb("wr_sb", [P, E], f32)
        rmsw = sb("rmsw", [P, 1], f32)
        ident = sb("ident", [P, P], f32)
        zeros = sb("zeros", [P, BANK], f32)
        empty_row = sb("empty_row", [P, SLOT_TILES], i32)
        ident_b = sb("ident_b", [P, P], bf16)
        mask_b = sb("mask_b", [P, P], bf16)
        stat = sb("stat", [P, 4, NT], f32)
        bias_e = sb("bias_e", [E, UP + D], f32)
        bias_r = sb("bias_r", [E, UP + D], f32)
        bias_s = sb("bias_s", [E, 3, UP + D], bf16)
        bias_rows = sb("bias_rows", [3, E * (UP + D)], bf16)
        bs_col = sb("bs_col", [P, 2, SB], f32)
        bs2_all = sb("bs2_all", [P, D], f32)
        ones3 = sb("ones3", [3, P], bf16)
        ones_b = sb("ones_b", [P, P], bf16)
        tri_b = sb("tri_b", [P, P], bf16)
        attn = ExitStack()
        tT = sb("tT", [P, N], f32, attn)
        q_hl = [sb(f"q_hl{h}", [P, N], f32r, attn) for h in range(2)]
        k_h = [sb(f"k_h{h}", [P, N], f32r, attn) for h in range(2)]
        k_l = [sb(f"k_l{h}", [P, N], f32r, attn) for h in range(2)]
        v_sb = sb("v_sb", [P, NT, P], f32, attn)
        probs = [[sb(f"probs{b}{h}", [P, N], f32, attn) for h in range(2)] for b in range(2)]
        xn = probs[0][0][:, :].rearrange("p (n d) -> p n d", d=D)
        probsT = [[sb(f"probsT{b}{h}", [P, NT, P], f32, attn) for h in range(2)] for b in range(2)]
        wqk_d = sb("wqk_d", [P, 4, 2, DH], f32, attn)
        wo_p = sb("wo_p", [P, D], f32, attn)
        outT = [[sb(f"outT{b}{h}", [P, P], f32, attn) for h in range(2)] for b in range(2)]
        gate1 = sb("gate1", [P, NT, HEADS], f32, attn)
        cmax = sb("cmax", [P, 2, NC], f32, attn)
        nmax = sb("nmax", [P, 2 * NT], f32, attn)
        rsum = sb("rsum", [P, 2 * NT], f32, attn)
        rden = sb("rden", [P, 2, 2], f32, attn)
        attn.close()
        moe = ExitStack()
        xT = sb("xT", [P, N], f32, moe)
        w_up = sb("w_up", [P, E, UP], f32, moe)
        w_down = sb("w_down", [P, E, HB, D], f32, moe)
        shared = sb("shared", [P, NT, D], f32, moe)
        logits = sb("logits", [P, NT, E], f32, moe)
        top8 = sb("top8", [P, NT, 8], f32, moe)
        idx8 = sb("idx8", [P, NT, 8], u32, moe)
        idxf = sb("idxf", [P, TOPK, NT], f32, moe)
        ie = sb("ie", [P, NT, E], f32, moe)
        hot = sb("hot", [P, TOPK, NT, E], f32, moe)
        routed = sb("routed", [P, NT * E], bf16, moe)
        rank = sb("rank", [P, NT, E], f32, moe)
        before = sb("before", [P, NT + 1, E], f32, moe)
        cnt_i = sb("cnt_i", [P, E], i32, moe)
        tiles_a = sb("tiles_a", [P, E], f32, moe)
        tiles_b = sb("tiles_b", [P, E], f32, moe)
        tiles_n = sb("tiles_n", [P, E], f32, moe)
        base = sb("base", [P, E], f32, moe)
        picked = sb("picked", [P, TOPK, NT, E], f32, moe)
        slot_f = sb("slot_f", [P, TOPK, NT], f32, moe)
        slot = sb("slot", [P, TOPK, NT], u32, moe)
        it = sb("it", [1, SLOT_TILES, E], f32, moe)
        past = sb("past", [1, SLOT_TILES, E], f32, moe)
        exp_f = sb("exp_f", [1, SLOT_TILES], f32, moe)
        exp_i = sb("exp_i", [1, SLOT_TILES], i32, moe)
        gat = sb("gat", [P, 4, NT], f32, moe)
        bn = sb("bn", [P, NT, 6], f32, moe)
        mv = sb("mv", [P, NT, 2], f32, moe)
        rstd = sb("rstd", [P, 2, NT], f32, moe)
        sil_s = sb("sil_s", [P, 2, BANK], f32, moe)
        act_s = sb("act_s", [P, 2, SB, BANK], f32, moe)
        rows = sb("rows", [P, TOPK, NT, D + 1], f32, moe)
        xg = sb("xg", [P, 2, D + 1], f32, moe)
        row_all = sb("row_all", [P, SLOT_TILES], i32, moe)
        row_now = sb("row_now", [P, 2], u32, moe)
        xgT = sb("xgT", [P, 2, P], f32, moe)
        sil = sb("sil", [P, 2, H], f32, moe)
        hid = sb("hid", [P, 2, H], f32, moe)
        hidT = sb("hidT", [P, 2, H], f32, moe)
        y_sb = sb("y_sb", [P, 2, D], f32, moe)
        yg = sb("yg", [P, TOPK, NT, D], f32, moe)
        fin = sb("fin", [P, NT, D], f32, moe)
        moe.close()

        x_sorted = nc.dram_tensor("x_sorted", (SLOTS, D + 1), f32, kind="Internal").ap()
        y_rows = nc.dram_tensor("y_rows", (TOPK * N + SLOTS, D), f32, kind="Internal").ap()

        def bank(name):
            return ctx.enter_context(nc.psum_tensor(name, [P, BANK], f32))

        ps_s = [bank(f"ps_s{i}") for i in range(RING)]
        ps_t = [bank(f"ps_t{i}") for i in range(2)]
        ps_pv = bank("ps_pv")
        ps_wo = bank("ps_wo")

        x_in, w_in, wo_in, gw_in = sem("x_in"), sem("w_in"), sem("wo_in"), sem("gw_in")
        moe_in, shw_in, bias_in, brow_in = sem("moe_in"), sem("shw_in"), sem("bias_in"), sem("brow_in")
        out_done = sem("out_done")
        zero_set, zfill, consts, ident_set = sem("zero_set"), sem("zfill"), sem("consts"), sem("ident_set")
        pool_step = sem("pool_step")
        dve_step, act_step = sem("dve_step"), sem("act_step")
        bias_split = sem("bias_split")
        ms_ready, std_ready, xn_ready, xnT_ready, tT_ready = (sem(n) for n in (
            "ms_ready", "std_ready", "xn_ready", "xnT_ready", "tT_ready"))
        z_ready, ez_ready, gate_ready = sem("z_ready"), sem("ez_ready"), sem("gate_ready")
        pair_w, fill, freed, high = sem("pair_w"), sem("fill"), sem("freed"), sem("high")
        row_max, exp_done = sem("row_max"), sem("exp_done")
        turned, moved0, moved1 = sem("turned"), sem("moved0"), sem("moved1")
        pv_done, out_ready, wo_done, acc_done = sem("pv_done"), sem("out_ready"), sem("wo_done"), sem("acc_done")
        loop_step = sem("loop_step")
        var_ready, ln_std, x1_ready = sem("var_ready"), sem("ln_std"), sem("x1_ready")
        x1T_psum, x1T_ready = sem("x1T_psum"), sem("x1T_ready")
        lg_psum, lg_ready, gexp = sem("lg_psum"), sem("lg_ready"), sem("gexp")
        routed_ready, count_psum, slots_ready, expert_ready = (sem(n) for n in (
            "routed_ready", "count_psum", "slots_ready", "expert_ready"))
        scattered, rows_ready = sem("scattered"), sem("rows_ready")
        row_noted, row_set, sent = sem("row_noted"), sem("row_set"), sem("sent")
        yg_in = [sem(f"yg_in{c}") for c in range(NC)]
        up_s, sil_done, act_done, down_s, shared_done = (sem(n) for n in (
            "up_s", "sil_done", "act_done", "down_s", "shared_done"))
        xg_in = [sem(f"xg_in{b}") for b in range(2)]
        y_out = [sem(f"y_out{b}") for b in range(2)]
        xgT_psum, xgT_ready, up_e, sil_e, hid_e = (sem(n) for n in (
            "xgT_psum", "xgT_ready", "up_e", "sil_e", "hid_e"))
        hidT_psum, hidT_ready, down_e, y_ready = (sem(n) for n in (
            "hidT_psum", "hidT_ready", "down_e", "y_ready"))
        fin_var, fin_std, fin_ready = sem("fin_var"), sem("fin_std"), sem("fin_ready")

        def loaded(n, b):
            return (n + (2 - b)) * 8

        def expert_slots(engine, slot):
            slot(-1, 1, up=False, turn_hidden=False, down=False)
            slot(0, 0, turn_hidden=False, down=False)
            slot(1, 1, down=False)
            slot(2, 0)
            slot(3, 1)
            with engine.Fori(2, SLOT_TILES // 2 - 1) as i:
                for b in range(2):
                    slot(i * 2 + b, b)
            n = SLOT_TILES
            slot(n - 2, 0)
            slot(n - 1, 1, turn_next=False)
            slot(n, 0, up=False, turn_next=False)
            slot(n + 1, 1, up=False, turn_next=False, turn_hidden=False)

        ONE = 1

        block = ctx.enter_context(nc.Block())

        @block.sync
        def _(sp):
            for s in (wo_done, pv_done, turned, freed, moved0, moved1, out_ready, acc_done):
                sp.sem_inc(s, ONE)
            sp.dma_start(x_acc[:, :, :], tokens[0].rearrange("(n p) d -> p n d", p=P)).then_inc(x_in, 16)
            sp.dma_start(rmsw[:, :], rms_w.rearrange("(p a) -> p a", a=1)).then_inc(gw_in, 16)
            sp.dma_start(wgate_sb[:, :], w_gates).then_inc(gw_in, 16)
            sp.dma_start(wr_sb[:, :], Wg).then_inc(gw_in, 16)
            sp.dma_start(wq_sb[:, :, :], wq.rearrange("h d e -> d h e")).then_inc(w_in, 16)
            sp.dma_start(wk_sb[:, :, :], wk.rearrange("h d e -> d h e")).then_inc(w_in, 16)
            sp.dma_start(wv_sb[:, :].rearrange("d (h e) -> d h e", h=HEADS),
                         wv.rearrange("h d e -> d h e")).then_inc(w_in, 16)
            sp.dma_start(wo_sb[:, :, :], wo.rearrange("(n a) e d -> (a e) n d", a=2)).then_inc(wo_in, 16)
            sp.dma_start(bias_e[:, 0:H], b1).then_inc(bias_in, 16)
            sp.dma_start(bias_e[:, H:UP], b11).then_inc(bias_in, 16)
            sp.dma_start(bias_e[:, UP:], b2).then_inc(bias_in, 16)
            with nc.allow_non_contiguous_dma("a column of biases on each partition, 1 KB"):
                sp.dma_start(bs_col[:, 0, :], bs1.rearrange("(m p) -> p m", p=P)).then_inc(shw_in, 16)
                sp.dma_start(bs_col[:, 1, :], bs11.rearrange("(m p) -> p m", p=P)).then_inc(shw_in, 16)
            sp.dma_start(bs2_all[:, :], bs2.rearrange("(a d) -> a d", a=1).to_broadcast([P, D])).then_inc(shw_in, 16)
            sp.dma_start(ws_up[:, 0, :], Ws1).then_inc(shw_in, 16)
            sp.dma_start(ws_up[:, 1, :], Ws11).then_inc(shw_in, 16)
            sp.dma_start(ws_down[:, :, :], Ws2.rearrange("(m p) d -> p m d", p=P)).then_inc(shw_in, 16)
            sp.wait_ge(zero_set, 2)
            view = x_sorted.rearrange("(g n p) d -> g p n d", p=P, n=BT)
            for g in range(SLOT_TILES // BT):
                sp.dma_start(view[g, :, :, 0:D], zeros[:, :].rearrange("p (n d) -> p n d", d=D)).then_inc(zfill, 16)
            with nc.allow_non_contiguous_dma("one number of each row, 24 KB"):
                sp.dma_start(x_sorted.rearrange("(n p) d -> p n d", p=P)[:, :, D].bitcast(i32),
                             empty_row[:, :]).then_inc(zfill, 16)
            sp.wait_ge(bias_split, 1)
            for k in range(3):
                sp.dma_start(bias_rows[k:k + 1, :].rearrange("a (e n) -> a e n", e=E),
                             bias_s[:, k, :]).then_inc(brow_in, 16)
            sp.wait_ge(acc_done, ONE + PAIRS * NT)
            sp.dma_start(w_up[:, :, 0:H], W1.rearrange("e d h -> d e h")).then_inc(moe_in, 16)
            sp.dma_start(w_up[:, :, H:], W11.rearrange("e d h -> d e h")).then_inc(moe_in, 16)
            sp.dma_start(w_down[:, :, :, :], W2.rearrange("e (m p) d -> p e m d", p=P)).then_inc(moe_in, 16)
            sp.wait_ge(scattered, 16 * TOPK * NT)
            for b in range(2):
                sp.dma_start(xg[:, b, :], x_sorted[b * P:(b + 1) * P, :]).then_inc(xg_in[b], 16)
            with sp.Fori(1, SLOT_TILES // 2) as i:
                for b in range(2):
                    sp.wait_ge(xgT_psum, i * 2 + (b - 1))
                    sp.wait_ge(row_noted, i * 2 + (b - 1))
                    sp.dma_start(xg[:, b, :], x_sorted[bass.ds(i * (2 * P) + b * P, P), :]).then_inc(xg_in[b], 16)
            for b in range(2):
                sp.wait_ge(y_out[b], 16 * (SLOT_TILES // 2))
            for c in range(NC):
                for k in range(TOPK):
                    at = k * N + c * BANK
                    sp.dma_start(yg[:, k, c * BT:(c + 1) * BT, :],
                                 y_rows[at:at + BANK, :].rearrange("(n p) d -> p n d", p=P)).then_inc(yg_in[c], 16)
            for c in range(NC):
                sp.wait_ge(fin_ready, BT * (c + 1))
                sp.dma_start(out[0, c * BANK:(c + 1) * BANK, :].rearrange("(n p) d -> p n d", p=P),
                             fin[:, c * BT:(c + 1) * BT, :]).then_inc(out_done, 16)
            sp.wait_ge(out_done, 16 * NC)

        @block.gpsimd
        def _(pool):
            nc.gpsimd.memset(ident[:, :], 0.0).then_inc(pool_step, 1)
            nc.gpsimd.memset(mask_b[:, :], 0.0).then_inc(pool_step, 1)
            nc.gpsimd.memset(tri_b[:, :], 1.0).then_inc(pool_step, 1)
            nc.gpsimd.memset(ones_b[:, :], 1.0).then_inc(consts, 1)
            nc.gpsimd.memset(ones3[:, :], 1.0).then_inc(consts, 1)
            nc.gpsimd.memset(zeros[:, :], 0.0).then_inc(zero_set, 1)
            for b in range(2):
                for h in range(2):
                    nc.gpsimd.memset(outT[b][h][:, :], 0.0).then_inc(consts, 1)
            nc.gpsimd.memset(ident_b[:, :], 0.0).then_inc(pool_step, 1)
            nc.gpsimd.iota(empty_row[:, :], pattern=[[P, SLOT_TILES]], base=TOPK * N,
                           channel_multiplier=1).then_inc(zero_set, 1)
            pool.wait_ge(pool_step, 4)
            nc.gpsimd.affine_select(out=ident[:, :], in_=ident[:, :], compare_op=ALU.not_equal, fill=1.0,
                                    base=0, pattern=[[-1, P]], channel_multiplier=1).then_inc(ident_set, 1)
            nc.gpsimd.affine_select(out=ident_b[:, :], in_=ident_b[:, :], compare_op=ALU.not_equal, fill=1.0,
                                    base=0, pattern=[[-1, P]], channel_multiplier=1).then_inc(ident_set, 1)
            nc.gpsimd.affine_select(out=mask_b[:, :], in_=mask_b[:, :], compare_op=ALU.is_ge,
                                    fill=MASKED, base=0, pattern=[[-1, P]], channel_multiplier=1).then_inc(consts, 1)
            nc.gpsimd.affine_select(out=tri_b[:, :], in_=tri_b[:, :], compare_op=ALU.is_gt, fill=0.0,
                                    base=0, pattern=[[1, P]], channel_multiplier=-1).then_inc(consts, 1)
            pool.wait_ge(w_in, 48)
            pool.wait_ge(wo_in, 16)
            with pool.Fori(0, PAIRS) as p:
                pool.wait_ge(wo_done, ONE + p * NT)
                for n, w in enumerate((wq_sb, wk_sb)):
                    nc.gpsimd.tensor_copy(wqk_d[:, 2 * n:2 * n + 2, 0, :],
                                          w[:, bass.ds(p * 2, 2), :]).then_inc(pair_w, 1)
                    nc.gpsimd.tensor_copy(wqk_d[:, 2 * n:2 * n + 2, 1, :],
                                          w[:, bass.ds(p * 2, 2), :]).then_inc(pair_w, 1)
                nc.gpsimd.tensor_copy(wo_p[:, :], wo_sb[:, bass.ds(p, 1), :]
                                      .rearrange("d a e -> d (a e)")).then_inc(pair_w, 1)
            pool.wait_ge(acc_done, ONE + PAIRS * NT)
            nc.gpsimd.iota(ie[:, :, :], pattern=[[0, NT], [1, E]], base=0, channel_multiplier=0,
                           allow_small_or_imprecise_dtypes=True).then_inc(pool_step, 1)
            nc.gpsimd.iota(it[:, :, :], pattern=[[1, SLOT_TILES], [0, E]], base=0, channel_multiplier=0,
                           allow_small_or_imprecise_dtypes=True).then_inc(pool_step, 1)
            nc.gpsimd.iota(rows[:, :, :, D].bitcast(i32), pattern=[[N, TOPK], [P, NT]], base=0,
                           channel_multiplier=1).then_inc(pool_step, 1)
            pool.wait_ge(pool_step, 7)
            pool.wait_ge(zfill, 16 * (SLOT_TILES // BT + 1))
            pool.wait_ge(rows_ready, 1)
            pool.wait_ge(slots_ready, 1)
            for t in range(NT):
                for k in range(TOPK):
                    nc.gpsimd.indirect_dma_start(
                        out=x_sorted, out_offset=bass.IndirectOffsetOnAxis(ap=slot[:, k, t:t + 1], axis=0),
                        in_=rows[:, k, t, :], in_offset=None).then_inc(scattered, 16)
            def send(n, b):
                pool.wait_ge(row_noted, n + 1)
                nc.gpsimd.tensor_copy(row_now[:, b:b + 1], row_all[:, bass.ds(n, 1)]).then_inc(row_set, 1)
                pool.wait_ge(row_set, n + 1)
                pool.wait_ge(y_ready, n + 1)
                pool.sem_inc(sent, 1)
                nc.gpsimd.indirect_dma_start(
                    out=y_rows, out_offset=bass.IndirectOffsetOnAxis(ap=row_now[:, b:b + 1], axis=0),
                    in_=y_sb[:, b, :], in_offset=None).then_inc(y_out[b], 16)

            for b in range(2):
                send(b, b)
            with pool.Fori(1, SLOT_TILES // 2) as i:
                for b in range(2):
                    pool.wait_ge(y_out[b], i * 16)
                    send(i * 2 + b, b)

        @block.scalar
        def _(act):
            act.wait_ge(ms_ready, 1)
            nc.scalar.activation(stat[:, 1, :], stat[:, 0, :], ACT.Sqrt).then_inc(std_ready, 1)
            act.wait_ge(z_ready, 1)
            nc.scalar.activation(gate1[:, :, :].rearrange("p n h -> p (n h)"), ps_t[0][:, 0:NT * HEADS], ACT.Exp,
                                 scale=-1.0).then_inc(ez_ready, 1)

            with act.Fori(0, PAIRS) as p:
                for n in range(QK_FILLS):
                    w, c = n // NC, n % NC
                    act.wait_ge(fill, p * FILLS + (n + 1))
                    dst = q_hl[w] if w < 2 else k_h[w - 2]
                    nc.scalar.activation(dst[:, c * BANK:(c + 1) * BANK], ps_s[n % RING][:, :],
                                         ACT.Copy).then_inc(high, 1)

                def exps(s, h):
                    w = (ORDER[s] + 1) * P
                    row = slice(2 * s + h, 2 * s + h + 1)
                    act.wait_ge(row_max, p * (2 * NT) + (2 * s + h + 1))
                    nc.scalar.activation(probs[s % 2][h][:, 0:w], probs[s % 2][h][:, 0:w], ACT.Exp,
                                         bias=nmax[:, row], scale=SCALE,
                                         accum_out=rsum[:, row]).then_inc(exp_done, 1)

                def move(s, h, c, w):
                    g = first[s, h] + c
                    if g % 2 == 0:
                        if s >= 2:
                            act.wait_ge(pv_done, p * NT + (ONE + s - 1))
                        act.wait_ge(turned, p * GROUPS + (ONE + g + 1))
                        nc.scalar.activation(
                            probsT[s % 2][h][:, c * BT:c * BT + w // P, :].rearrange("p n i -> p (n i)"),
                            ps_t[0][:, 0:w], ACT.Copy).then_inc(moved0, 1)

                def unload(s):
                    act.wait_ge(pv_done, p * NT + (ONE + s + 1))
                    act.wait_ge(wo_done, p * NT + (ONE + max(s - 1, 0)))
                    for h in range(2):
                        rows = slice(h * DH, (h + 1) * DH)
                        nc.scalar.activation(outT[s % 2][h][rows, :], ps_pv[rows, 0:P], ACT.Copy).then_inc(out_ready, 1)

                for units in STEPS:
                    for stage, s, h, c, w in units:
                        last = (c, w) == chunks[s][-1]
                        if stage == "scores" and last:
                            exps(s, h)
                        elif stage == "turn":
                            move(s, h, c, w)
                        elif stage == "times_v" and last:
                            unload(s)

            act.wait_ge(var_ready, 1)
            nc.scalar.activation(rstd[:, 0, :], rstd[:, 1, :], ACT.Sqrt).then_inc(ln_std, 1)
            act.wait_ge(x1_ready, NT)
            nc.scalar.activation(rows[:, 1, :, 0:D], rows[:, 0, :, 0:D], ACT.Copy).then_inc(rows_ready, 1)
            act.wait_ge(gexp, 1)
            nc.scalar.activation(gat[:, 1, :], gat[:, 0, :], ACT.Exp).then_inc(gexp, 1)
            act.wait_ge(shw_in, 16 * 6)
            for c in range(NC):
                for m in range(SB):
                    n = c * SB + m
                    act.wait_ge(up_s, n + 1)
                    if n >= 2:
                        act.wait_ge(act_done, n - 1)
                    nc.scalar.activation(sil_s[:, n % 2, :], ps_s[2 * (n % 2)][:, :], ACT.Silu,
                                         bias=bs_col[:, 0, m:m + 1]).then_inc(sil_done, 1)
            def expert_slot(n, b, up=True, turn_next=True, turn_hidden=True, down=True):
                o = 1 - b
                if up:
                    act.wait_ge(up_e, n + 1)
                    nc.scalar.activation(sil[:, b, :], ps_s[b][:, 0:H], ACT.Silu).then_inc(sil_e, 1)
                if turn_next:
                    act.wait_ge(xgT_psum, n + 2)
                    nc.scalar.activation(xgT[:, o, :], ps_t[o][:, 0:P], ACT.Copy).then_inc(xgT_ready, 1)
                if down:
                    if not isinstance(n, int) or n >= 4:
                        act.wait_ge(y_out[b], loaded(n - 4, b))
                    act.wait_ge(down_e, n - 1)
                    nc.scalar.activation(y_sb[:, b, :], (ps_pv, ps_wo)[b][:, 0:D], ACT.Copy).then_inc(y_ready, 1)

            expert_slots(act, expert_slot)
            for c in range(NC):
                cols = slice(c * BT, (c + 1) * BT)
                act.wait_ge(fin_var, c + 1)
                nc.scalar.activation(rstd[:, 0, cols], rstd[:, 1, cols], ACT.Sqrt).then_inc(fin_std, 1)

        @block.vector
        def _(dve):
            steps = [0]

            def link(ins):
                steps[0] += 1
                ins.then_inc(dve_step, 1)
                dve.wait_ge(dve_step, steps[0])

            dve.wait_ge(x_in, 16)
            for t in range(NT):
                ins = nc.vector.tensor_tensor_reduce(out=xn[:, t, :], in0=x_acc[:, t, :], in1=x_acc[:, t, :],
                                                     scale=1.0 / D, scalar=RMS_EPS, op0=ALU.mult, op1=ALU.add,
                                                     accum_out=stat[:, 0, t:t + 1])
            ins.then_inc(ms_ready, 1)
            dve.wait_ge(bias_in, 48)
            link(nc.vector.tensor_copy(bias_s[:, 0, :], bias_e[:, :]))
            link(nc.vector.tensor_tensor(bias_r[:, :], bias_e[:, :], bias_s[:, 0, :], ALU.subtract))
            link(nc.vector.tensor_copy(bias_s[:, 1, :], bias_r[:, :]))
            link(nc.vector.tensor_tensor(bias_e[:, :], bias_r[:, :], bias_s[:, 1, :], ALU.subtract))
            nc.vector.tensor_copy(bias_s[:, 2, :], bias_e[:, :]).then_inc(bias_split, 1)
            dve.wait_ge(std_ready, 1)
            link(nc.vector.reciprocal(stat[:, 2, :], stat[:, 1, :]))
            for t in range(NT):
                nc.vector.tensor_scalar(xn[:, t, :], x_acc[:, t, :], stat[:, 2, t:t + 1], None,
                                        ALU.mult).then_inc(xn_ready, 1)
            dve.wait_ge(gw_in, 48)
            for c in range(NC):
                dve.wait_ge(xnT_ready, c + 1)
                nc.vector.tensor_scalar(tT[:, c * BANK:(c + 1) * BANK], ps_s[c][:, :], rmsw[:, 0:1], None,
                                        ALU.mult).then_inc(tT_ready, 1)
            dve.wait_ge(ez_ready, 1)
            nc.vector.tensor_scalar(gate1[:, :, :], gate1[:, :, :], 1.0, None, ALU.add).then_inc(gate_ready, 1)
            dve.wait_ge(gate_ready, 1)
            dve.wait_ge(consts, 8)

            LINKS = 5 * NT
            with dve.Fori(0, PAIRS) as p:
                count = [0]

                def link_in(ins):
                    count[0] += 1
                    ins.then_inc(loop_step, 1)
                    dve.wait_ge(loop_step, p * LINKS + count[0])

                for n in range(QK_FILLS):
                    w, c = n // NC, n % NC
                    cols = slice(c * BANK, (c + 1) * BANK)
                    dve.wait_ge(high, p * QK_FILLS + (n + 1))
                    if w < 2:
                        nc.vector.tensor_tensor(q_hl[w][DH:, cols], ps_s[n % RING][DH:, :],
                                                q_hl[w][DH:, cols].bitcast(f32), ALU.subtract).then_inc(freed, 1)
                    else:
                        nc.vector.tensor_tensor(k_l[w - 2][:, cols], ps_s[n % RING][:, :],
                                                k_h[w - 2][:, cols].bitcast(f32), ALU.subtract).then_inc(freed, 1)
                for c in range(V_FILLS):
                    n = QK_FILLS + c
                    dve.wait_ge(fill, p * FILLS + (n + 1))
                    nc.vector.tensor_copy(v_sb[:, c * BT:(c + 1) * BT, :].rearrange("p n e -> p (n e)"),
                                          ps_s[n % RING][:, :]).then_inc(freed, 1)

                def scores(s, h, c, w):
                    n = first_fill(s, h) + c
                    if c == 0 and s >= 2:
                        dve.wait_ge(turned, p * GROUPS + (ONE + group_end(s - 2, h)))
                    dve.wait_ge(fill, p * FILLS + (n + 1))
                    nc.vector.tensor_scalar(
                        probs[s % 2][h][:, c * BANK:c * BANK + w], ps_s[n % RING][:, 0:w], 1.0, None,
                        ALU.mult, ALU.max, accum_out=cmax[:, h, c:c + 1]).then_inc(freed, 1)
                    if c == len(chunks[s]) - 1:
                        row = slice(2 * s + h, 2 * s + h + 1)
                        dve.wait_ge(freed, p * FILLS + (ONE + n + 1))
                        link_in(nc.vector.tensor_reduce(nmax[:, row], cmax[:, h, 0:c + 1], X, ALU.max, negate=True))
                        nc.vector.tensor_scalar(nmax[:, row], nmax[:, row], SCALE, None, ALU.mult).then_inc(row_max, 1)

                def move(s, h, c, w):
                    g = first[s, h] + c
                    if g % 2 == 1:
                        if s >= 2:
                            dve.wait_ge(pv_done, p * NT + (ONE + s - 1))
                        dve.wait_ge(turned, p * GROUPS + (ONE + g + 1))
                        nc.vector.tensor_copy(
                            probsT[s % 2][h][:, c * BT:c * BT + w // P, :].rearrange("p n i -> p (n i)"),
                            ps_t[1][:, 0:w]).then_inc(moved1, 1)

                def add(s):
                    t = ORDER[s]
                    dve.wait_ge(exp_done, p * (2 * NT) + (2 * s + 2))
                    r = rden[:, s % 2, :]
                    link_in(nc.vector.tensor_tensor(r, rsum[:, 2 * s:2 * s + 2],
                                                    gate1[:, t, bass.ds(p * 2, 2)], ALU.mult))
                    link_in(nc.vector.reciprocal(r, r))
                    dve.wait_ge(wo_done, p * NT + (ONE + s + 1))
                    link_in(nc.vector.scalar_tensor_tensor(
                        out=x_acc[:, t, :], in0=ps_wo[:, 0:D], scalar=rden[:, s % 2, 0:1], in1=x_acc[:, t, :],
                        op0=ALU.mult, op1=ALU.add))
                    nc.vector.scalar_tensor_tensor(
                        out=x_acc[:, t, :], in0=ps_wo[:, D:2 * D], scalar=rden[:, s % 2, 1:2], in1=x_acc[:, t, :],
                        op0=ALU.mult, op1=ALU.add).then_inc(acc_done, 1)

                for units in STEPS:
                    for stage, s, h, c, w in units:
                        if stage == "scores":
                            scores(s, h, c, w)
                        elif stage == "turn":
                            move(s, h, c, w)
                        elif stage == "times_wo":
                            add(s)
                assert count[0] == LINKS

            def statistics(src, tiles):
                for t in tiles:
                    ins = nc.vector.bn_stats(bn[:, t, :], src(t))
                link(ins)
                for t in tiles:
                    ins = nc.vector.bn_aggr(mv[:, t, :], bn[:, t, :])
                link(ins)

            dve.wait_ge(acc_done, ONE + PAIRS * NT)
            statistics(lambda t: x_acc[:, t, :], range(NT))
            nc.vector.tensor_scalar(rstd[:, 1, :], mv[:, :, 1], LN_EPS, None, ALU.add).then_inc(var_ready, 1)
            dve.wait_ge(ln_std, 1)
            link(nc.vector.reciprocal(rstd[:, 1, :], rstd[:, 0, :]))
            for t in range(NT):
                nc.vector.tensor_scalar(rows[:, 0, t, 0:D], x_acc[:, t, :], mv[:, t, 0:1], rstd[:, 1, t:t + 1],
                                        ALU.subtract, ALU.mult).then_inc(x1_ready, 1)
            for c in range(NC):
                dve.wait_ge(x1T_psum, c + 1)
                nc.vector.tensor_copy(xT[:, c * BANK:(c + 1) * BANK], ps_s[c][:, :]).then_inc(x1T_ready, 1)
            dve.wait_ge(lg_psum, 1)
            link(nc.vector.tensor_copy(logits[:, :, :].rearrange("p n e -> p (n e)"), ps_t[0][:, 0:NT * E]))
            for t in range(NT):
                ins = nc.vector.max(top8[:, t, :], logits[:, t, :])
            link(ins)
            for t in range(NT):
                ins = nc.vector.max_index(idx8[:, t, :], top8[:, t, :], logits[:, t, :])
            link(ins)
            for k in range(TOPK):
                ins = nc.vector.tensor_copy(idxf[:, k, :], idx8[:, :, k])
            link(ins)
            dve.wait_ge(pool_step, 6)
            for k in range(TOPK):
                ins = nc.vector.tensor_tensor(hot[:, k], ie[:, :, :],
                                              idxf[:, k, :].unsqueeze(2).to_broadcast([P, NT, E]), ALU.is_equal)
            link(ins)
            nc.vector.tensor_tensor(routed[:, :].rearrange("p (n e) -> p n e", e=E), hot[:, 0], hot[:, 1],
                                    ALU.add).then_inc(routed_ready, 1)
            nc.vector.tensor_tensor(gat[:, 0, :], top8[:, :, 1], top8[:, :, 0], ALU.subtract).then_inc(gexp, 1)
            dve.wait_ge(count_psum, 1)
            link(nc.vector.tensor_copy(rank[:, :, :].rearrange("p n e -> p (n e)"), ps_t[1][:, 0:NT * E]))
            link(nc.vector.memset(before[:, 0, :], 0.0))
            for t in range(NT):
                link(nc.vector.tensor_tensor(before[:, t + 1, :], before[:, t, :],
                                             ps_pv[:, t * E:(t + 1) * E], ALU.add))
            link(nc.vector.tensor_scalar(tiles_a[:, :], before[:, NT, :], float(P - 1), None, ALU.add))
            link(nc.vector.tensor_copy(cnt_i[:, :], tiles_a[:, :]))
            link(nc.vector.tensor_scalar(cnt_i[:, :], cnt_i[:, :], P.bit_length() - 1, None,
                                         ALU.logical_shift_right))
            link(nc.vector.tensor_copy(tiles_n[:, :], cnt_i[:, :]))
            link(nc.vector.tensor_copy(tiles_a[:, :], tiles_n[:, :]))
            src, dst, d = tiles_a, tiles_b, 1
            while d < E:
                link(nc.vector.tensor_copy(dst[:, 0:d], src[:, 0:d]))
                link(nc.vector.tensor_tensor(dst[:, d:], src[:, d:], src[:, 0:E - d], ALU.add))
                src, dst, d = dst, src, 2 * d
            link(nc.vector.tensor_tensor(base[:, :], src[:, :], tiles_n[:, :], ALU.subtract))
            link(nc.vector.tensor_scalar(base[:, :], base[:, :], float(P), None, ALU.mult))
            link(nc.vector.tensor_tensor(rank[:, :, :], rank[:, :, :], before[:, 0:NT, :], ALU.add))
            link(nc.vector.tensor_tensor(rank[:, :, :], rank[:, :, :],
                                         base[:, :].unsqueeze(1).to_broadcast([P, NT, E]), ALU.add))
            for k in range(TOPK):
                link(nc.vector.tensor_tensor(picked[:, k], hot[:, k], rank[:, :, :], ALU.mult))
                link(nc.vector.tensor_reduce(slot_f[:, k, :], picked[:, k], X, ALU.add))
            nc.vector.tensor_copy(slot[:, :, :], slot_f[:, :, :]).then_inc(slots_ready, 1)
            link(nc.vector.tensor_tensor(past[:, :, :], it[:, :, :],
                                         src[0:1, :].unsqueeze(1).to_broadcast([1, SLOT_TILES, E]), ALU.is_ge))
            link(nc.vector.tensor_reduce(exp_f[:, :], past[:, :, :], X, ALU.add))
            link(nc.vector.tensor_scalar(exp_f[:, :], exp_f[:, :], float(E - 1), None, ALU.min))
            nc.vector.tensor_copy(exp_i[:, :], exp_f[:, :]).then_inc(expert_ready, 1)
            dve.wait_ge(gexp, 2)
            link(nc.vector.tensor_scalar(gat[:, 2, :], gat[:, 1, :], 1.0, None, ALU.add))
            link(nc.vector.reciprocal(gat[:, 2, :], gat[:, 2, :]))
            link(nc.vector.tensor_tensor(gat[:, 3, :], gat[:, 1, :], gat[:, 2, :], ALU.mult))
            dve.wait_ge(shw_in, 16 * 6)
            for t in range(NT):
                ins = nc.vector.tensor_tensor(shared[:, t, :], rows[:, 0, t, 0:D], bs2_all[:, :], ALU.add)
            link(ins)

            def shared_add(c):
                dve.wait_ge(down_s, c + 1)
                sh = shared[:, c * BT:(c + 1) * BT, :].rearrange("p n d -> p (n d)")
                nc.vector.tensor_tensor(sh, ps_t[c % 2][:, :], sh, ALU.add).then_inc(shared_done, 1)

            for c in range(NC):
                for m in range(SB):
                    n = c * SB + m
                    dve.wait_ge(sil_done, n + 1)
                    if c >= 2 and m == 0:
                        dve.wait_ge(down_s, c - 1)
                    nc.vector.scalar_tensor_tensor(out=act_s[:, c % 2, m, :], in0=ps_s[2 * (n % 2) + 1][:, :],
                                                   scalar=bs_col[:, 1, m:m + 1], in1=sil_s[:, n % 2, :],
                                                   op0=ALU.add, op1=ALU.mult).then_inc(act_done, 1)
                if c >= 1:
                    shared_add(c - 1)
            shared_add(NC - 1)
            def expert_slot(n, b, up=True, turn_next=True, turn_hidden=True, down=True):
                o = 1 - b
                if turn_hidden:
                    dve.wait_ge(hidT_psum, n)
                    nc.vector.tensor_copy(hidT[:, o, :], ps_s[2 + o][:, 0:H]).then_inc(hidT_ready, 1)
                if turn_next:
                    dve.wait_ge(xg_in[o], loaded(n + 1, o))
                    nc.vector.tensor_copy(row_all[:, bass.ds(n + 1, 1)],
                                          xg[:, o, D:D + 1].bitcast(i32)).then_inc(row_noted, 1)
                if up:
                    dve.wait_ge(sil_e, n + 1)
                    nc.vector.tensor_tensor(hid[:, b, :], ps_s[b][:, H:UP], sil[:, b, :], ALU.mult).then_inc(hid_e, 1)

            expert_slots(dve, expert_slot)
            for c in range(NC):
                dve.wait_ge(yg_in[c], 16 * TOPK)
                tiles = range(c * BT, (c + 1) * BT)
                cols = slice(c * BT, (c + 1) * BT)
                for k in range(TOPK):
                    for t in tiles:
                        ins = nc.vector.scalar_tensor_tensor(out=shared[:, t, :], in0=yg[:, k, t, :],
                                                             scalar=gat[:, 2 + k, t:t + 1], in1=shared[:, t, :],
                                                             op0=ALU.mult, op1=ALU.add)
                    link(ins)
                statistics(lambda t: shared[:, t, :], tiles)
                nc.vector.tensor_scalar(rstd[:, 1, cols], mv[:, cols, 1], LN_EPS, None, ALU.add).then_inc(fin_var, 1)
                dve.wait_ge(fin_std, c + 1)
                link(nc.vector.reciprocal(rstd[:, 1, cols], rstd[:, 0, cols]))
                for t in tiles:
                    nc.vector.tensor_scalar(fin[:, t, :], shared[:, t, :], mv[:, t, 0:1], rstd[:, 1, t:t + 1],
                                            ALU.subtract, ALU.mult).then_inc(fin_ready, 1)

        @block.tensor
        def _(pe):
            def turn(dst, src):
                return nc.tensor.transpose(dst, src, ident[:, :])

            pe.wait_ge(ident_set, 1)
            for c in range(NC):
                pe.wait_ge(xn_ready, BT * (c + 1))
                for j in range(BT):
                    mm = turn(ps_s[c][:, j * P:(j + 1) * P], xn[:, c * BT + j, :])
                mm.then_inc(xnT_ready, 1)
            pe.wait_ge(gw_in, 48)
            pe.wait_ge(tT_ready, NC)
            for t in range(NT):
                mm = nc.tensor.matmul(ps_t[0][:, t * HEADS:(t + 1) * HEADS], tT[:, t * P:(t + 1) * P],
                                      wgate_sb[:, :], start=True, stop=True)
            mm.then_inc(z_ready, 1)
            pe.wait_ge(w_in, 48)
            pe.wait_ge(consts, 8)
            pe.wait_ge(ident_set, 2)
            pe.wait_ge(ez_ready, 1)

            with pe.Fori(0, PAIRS) as p:
                pe.wait_ge(pair_w, p * 5 + 5)

                def free_bank(n):
                    pe.wait_ge(freed, ONE + p * FILLS + max(n - RING + 1, 0))

                for n in range(QK_FILLS):
                    w, c = n // NC, n % NC
                    free_bank(n)
                    nc.tensor.matmul(ps_s[n % RING][:, :], wqk_d[:, w].rearrange("d a e -> d (a e)"),
                                     tT[:, c * BANK:(c + 1) * BANK], start=True, stop=True).then_inc(fill, 1)
                for c in range(V_FILLS):
                    n = QK_FILLS + c
                    free_bank(n)
                    for j in range(BT):
                        t = c * BT + j
                        mm = nc.tensor.matmul(ps_s[n % RING][:, j * P:(j + 1) * P], tT[:, t * P:(t + 1) * P],
                                              wv_sb[:, bass.ds(p * P, P)], start=True, stop=True)
                    mm.then_inc(fill, 1)
                pe.wait_ge(freed, ONE + p * FILLS + (QK_FILLS + V_FILLS))

                def scores(s, h, c, w):
                    n = first_fill(s, h) + c
                    t = ORDER[s]
                    free_bank(n)
                    q = q_hl[h][:, t * P:(t + 1) * P]
                    nc.tensor.matmul(ps_s[n % RING][:, 0:w], q, k_h[h][:, c * BANK:c * BANK + w],
                                     start=True, stop=False)
                    if c == len(chunks[s]) - 1:
                        nc.tensor.matmul(ps_s[n % RING][:, w - P:w], ident_b[:, :], mask_b[:, :],
                                         start=False, stop=False, skip_group_check=True)
                    nc.tensor.matmul(ps_s[n % RING][:, 0:w], q, k_l[h][:, c * BANK:c * BANK + w],
                                     start=False, stop=True).then_inc(fill, 1)

                def turn_probs(s, h, c, w):
                    g = first[s, h] + c
                    if c == 0:
                        pe.wait_ge(exp_done, p * (2 * NT) + (2 * s + h + 1))
                    pe.wait_ge((moved0, moved1)[g % 2], p * (GROUPS // 2) + (ONE + g // 2))
                    for j in range(w // P):
                        at = c * BANK + j * P
                        mm = turn(ps_t[g % 2][:, j * P:(j + 1) * P], probs[s % 2][h][:, at:at + P])
                    mm.then_inc(turned, 1)

                def times_v(s, c, w):
                    t = ORDER[s]
                    if c == 0:
                        done = group_end(s, 1)
                        pe.wait_ge(moved0, p * (GROUPS // 2) + (ONE + (done + 1) // 2))
                        pe.wait_ge(moved1, p * (GROUPS // 2) + (ONE + done // 2))
                        pe.wait_ge(out_ready, p * (2 * NT) + (ONE + 2 * s))
                    for j in range(c * BT, c * BT + w // P):
                        for h in range(2):
                            rows = slice(h * DH, (h + 1) * DH)
                            mm = nc.tensor.matmul(ps_pv[rows, 0:P], v_sb[:, j, rows], probsT[s % 2][h][:, j, :],
                                                  start=(j == 0), stop=(j == t))
                    if j == t:
                        mm.then_inc(pv_done, 1)

                def times_wo(s):
                    pe.wait_ge(out_ready, p * (2 * NT) + (ONE + 2 * s + 2))
                    pe.wait_ge(acc_done, p * NT + (ONE + s))
                    for h in range(2):
                        mm = nc.tensor.matmul(ps_wo[:, h * D:(h + 1) * D], outT[s % 2][h][:, :], wo_p[:, :],
                                              start=True, stop=True)
                    mm.then_inc(wo_done, 1)

                for units in STEPS:
                    for stage, s, h, c, w in units:
                        if stage == "scores":
                            scores(s, h, c, w)
                        elif stage == "turn":
                            turn_probs(s, h, c, w)
                        elif stage == "times_v":
                            times_v(s, c, w)
                        else:
                            times_wo(s)

            for c in range(NC):
                pe.wait_ge(x1_ready, BT * (c + 1))
                for j in range(BT):
                    mm = turn(ps_s[c][:, j * P:(j + 1) * P], rows[:, 0, c * BT + j, 0:D])
                mm.then_inc(x1T_psum, 1)
            pe.wait_ge(x1T_ready, NC)
            for t in range(NT):
                mm = nc.tensor.matmul(ps_t[0][:, t * E:(t + 1) * E], xT[:, t * P:(t + 1) * P], wr_sb[:, :],
                                      start=True, stop=True)
            mm.then_inc(lg_psum, 1)
            pe.wait_ge(routed_ready, 1)
            nc.tensor.matmul(ps_t[1][:, 0:NT * E], tri_b[:, :], routed[:, :], start=True, stop=True)
            nc.tensor.matmul(ps_pv[:, 0:NT * E], ones_b[:, :], routed[:, :], start=True, stop=True).then_inc(count_psum, 1)
            pe.wait_ge(shw_in, 16 * 6)

            def shared_down(c):
                pe.wait_ge(act_done, SB * (c + 1))
                if c >= 2:
                    pe.wait_ge(shared_done, c - 1)
                for j in range(BT):
                    for m in range(SB):
                        mm = nc.tensor.matmul(ps_t[c % 2][:, j * P:(j + 1) * P],
                                              act_s[:, c % 2, m, j * P:(j + 1) * P], ws_down[:, m, :],
                                              start=(m == 0), stop=(m == SB - 1))
                mm.then_inc(down_s, 1)

            pe.wait_ge(slots_ready, 1)
            for c in range(NC):
                for m in range(SB):
                    n = c * SB + m
                    if n >= 2:
                        pe.wait_ge(act_done, n - 1)
                    for a in range(2):
                        mm = nc.tensor.matmul(ps_s[2 * (n % 2) + a][:, :], ws_up[:, a, m * P:(m + 1) * P],
                                              xT[:, c * BANK:(c + 1) * BANK], start=True, stop=True)
                    mm.then_inc(up_s, 1)
                if c >= 1:
                    shared_down(c - 1)
            shared_down(NC - 1)
            pe.wait_ge(moe_in, 48)
            pe.wait_ge(brow_in, 48)
            pe.wait_ge(expert_ready, 1)
            pe.wait_ge(shared_done, NC)

            def expert_of(n):
                return pe.value_load(exp_i[0:1, bass.ds(n, 1)], min_val=0, max_val=E - 1)

            def expert_slot(n, b, up=True, turn_next=True, turn_hidden=True, down=True):
                o = 1 - b
                start = isinstance(n, int) and n < 2 + b
                if up:
                    e = expert_of(n)
                    pe.wait_ge(xgT_ready, n + 1)
                    if not start:
                        pe.wait_ge(hid_e, n - 1)
                    nc.tensor.matmul(ps_s[b][:, :], ones3[:, :], bias_rows[:, bass.ds(e * (UP + D), UP)],
                                     start=True, stop=False)
                    nc.tensor.matmul(ps_s[b][:, :], xgT[:, b, :],
                                     w_up[:, bass.ds(e, 1), :].rearrange("p a n -> p (a n)"),
                                     start=False, stop=True).then_inc(up_e, 1)
                if turn_hidden:
                    pe.wait_ge(hid_e, n)
                    if not isinstance(n, int) or n >= 3:
                        pe.wait_ge(hidT_ready, n - 2)
                    for m in range(HB):
                        mm = turn(ps_s[2 + o][:, m * P:(m + 1) * P], hid[:, o, m * P:(m + 1) * P])
                    mm.then_inc(hidT_psum, 1)
                if turn_next:
                    pe.wait_ge(xg_in[o], loaded(n + 1, o))
                    if not isinstance(n, int) or n >= 1:
                        pe.wait_ge(xgT_ready, n)
                    turn(ps_t[o][:, 0:P], xg[:, o, 0:D]).then_inc(xgT_psum, 1)
                if down:
                    e = expert_of(n - 2)
                    pe.wait_ge(hidT_ready, n - 1)
                    if not isinstance(n, int) or n >= 4:
                        pe.wait_ge(y_ready, n - 3)
                    y = (ps_pv, ps_wo)[b][:, 0:D]
                    nc.tensor.matmul(y, ones3[:, :], bias_rows[:, bass.ds(e * (UP + D) + UP, D)],
                                     start=True, stop=False)
                    for m in range(HB):
                        mm = nc.tensor.matmul(y, hidT[:, b, m * P:(m + 1) * P],
                                              w_down[:, bass.ds(e, 1), m, :].rearrange("p a n -> p (a n)"),
                                              start=False, stop=(m == HB - 1))
                    mm.then_inc(down_e, 1)

            expert_slots(pe, expert_slot)


_INS = ['L0_attn_tokens', 'L0_attn_wq', 'L0_attn_wk', 'L0_attn_wv', 'L0_attn_wo', 'L0_attn_w_gates', 'L0_attn_rms_w',
        'L0_ffn_Wg', 'L0_ffn_W1', 'L0_ffn_b1', 'L0_ffn_W11', 'L0_ffn_b11', 'L0_ffn_W2', 'L0_ffn_b2',
        'L0_ffn_Ws1', 'L0_ffn_bs1', 'L0_ffn_Ws11', 'L0_ffn_bs11', 'L0_ffn_Ws2', 'L0_ffn_bs2']


def kernel(**inputs):
    import numpy as _np
    import concourse.bacc as _bacc
    from concourse import mybir as _mybir
    from concourse.bass_utils import run_bass_kernel_spmd as _run

    nc = _bacc.Bacc("TRN2", target_bir_lowering=False, num_devices=1)
    arrays, aps = {}, {}
    for name in _INS:
        a = _np.ascontiguousarray(inputs[name])
        arrays[f"in_{name}"] = a
        short = name.replace("L0_attn_", "").replace("L0_ffn_", "")
        aps[short] = nc.dram_tensor(f"in_{name}", a.shape, _mybir.dt.from_np(a.dtype), kind="ExternalInput").ap()
    aps["out"] = nc.dram_tensor("out_0", (1, 2048, 128), _mybir.dt.float32, kind="ExternalOutput").ap()
    attention_moe_layer(nc, **aps)
    r = _run(nc, [arrays], core_ids=[0])
    return r.results[0]["out_0"]
```

```python
import concourse.bass as bass
from concourse import mybir
from contextlib import ExitStack


def attention_moe_layer(nc, tokens, wq, wk, wv, wo, w_gates, rms_w, Wg, W1, b1, W11, b11, W2, b2,
                        Ws1, bs1, Ws11, bs11, Ws2, bs2, out):
    f32, f32r, bf16 = mybir.dt.float32, mybir.dt.float32r, mybir.dt.bfloat16
    i32, u32 = mybir.dt.int32, mybir.dt.uint32
    ALU, ACT, X = mybir.AluOpType, mybir.ActivationFunctionType, mybir.AxisListType.X

    P = 128
    N, D = tokens.shape[1], tokens.shape[2]
    HEADS, DH = wq.shape[0], wq.shape[2]
    E, H = W1.shape[0], W1.shape[2]
    HS = Ws1.shape[1]
    NT = N // P
    PAIRS = HEADS // 2
    BANK = 512
    BT = BANK // P
    NC = N // BANK
    TOPK = 2
    UP = 2 * H
    HB = H // P
    SB = HS // P
    SLOT_TILES = TOPK * N // P + E
    SLOTS = SLOT_TILES * P
    ROUND = 4
    ROUNDS = SLOT_TILES // ROUND + 1
    IDS = 8
    RMS_EPS = 2.0 ** -23
    LN_EPS = 1e-5
    SCALE = DH ** -0.5
    MASKED = -1e30

    ORDER = list(range(0, NT, 2)) + list(reversed(range(1, NT, 2)))
    chunks = [[(c, min(BANK, (t + 1) * P - c * BANK)) for c in range(t // BT + 1)] for t in ORDER]
    GROUPS = 2 * sum(len(c) for c in chunks)
    PROJECTIONS = 3 * NC
    FILLS = GROUPS + PROJECTIONS
    KQ_FILLS = PROJECTIONS - NC
    FREED = FILLS - NC
    RING = 4
    K, Q, V = range(3)
    first = {}
    for s in range(NT):
        for h in range(2):
            first[s, h] = 2 * sum(len(c) for c in chunks[:s]) + h * len(chunks[s])

    def group_end(s, h):
        return first[s, h] + len(chunks[s])

    last_use = [max(s for s in range(NT) if ORDER[s] // BT >= c) for c in range(NC)]
    project_at = {NT: [(K, 3), (K, 2), (K, 1), (K, 0)], NT + 1: [(Q, 3), (Q, 2), (Q, 1), (Q, 0), (V, 3)],
                  NT + 2: [(V, 2), (V, 1), (V, 0)]}

    NORM_ORDER = sorted(range(NC), key=lambda c: max(s for s in range(NT) if ORDER[s] // BT == c))
    summed = [max(s for s in range(NT) if ORDER[s] // BT == c) + 1 for c in range(NC)]
    n0, n1, n2, n3 = NORM_ORDER
    norm_at = {NT: [("stats", n0), ("stats", n1)], NT + 1: [("norm", n0), ("norm", n1), ("stats", n2)]}

    def step_units(s, project):
        units = []
        if s < NT:
            units += [("scores", s, h, c, w) for h in range(2) for c, w in chunks[s]]
        stages = [units]
        if 1 <= s <= NT:
            stages.append([("turn", s - 1, h, c, w) for h in range(2) for c, w in chunks[s - 1]])
        if 2 <= s < NT + 2:
            stages.append([("times_v", s - 2, 0, c, w) for c, w in chunks[s - 2]])
        if s >= 3:
            stages.append([("times_wo", s - 3, 0, 0, 0)])
        if project:
            stages.append([("project", w, 0, c, 0) for w, c in project_at.get(s, [])])
        else:
            stages.append([(stage, 0, 0, c, 0) for stage, c in norm_at.get(s, [])])
        placed = [((i + 0.5) / len(u), k, x) for k, u in enumerate(stages) for i, x in enumerate(u)]
        return [x for _, _, x in sorted(placed, key=lambda y: y[:2])]

    START = [("project", w, 0, c, 0) for c in range(NC) for w in (K, Q)] + [("project", V, 0, c, 0) for c in range(NC)]
    fork = min(project_at)
    HEAD = [x for s in range(fork) for x in step_units(s, False)]
    MORE = [x for s in range(fork, NT + 3) for x in step_units(s, True)]
    LAST = [x for s in range(fork, NT + 3) for x in step_units(s, False)] + [("turn_x", 0, 0, c, 0) for c in (n0, n1)]

    def numbered(units, stages):
        return {x: n for n, x in enumerate(x for x in units if x[0] in stages)}

    fill_of = numbered(HEAD + MORE, ("scores", "project"))
    last_fill_of = numbered(HEAD + LAST, ("scores", "project"))
    start_fill_of = numbered(START, ("project",))
    high_of = {x: n for n, x in enumerate(x for x in MORE if x[0] == "project" and x[1] != V)}
    start_high_of = {x: n for n, x in enumerate(x for x in START if x[1] != V)}

    def started(*unit):
        return unit, start_fill_of[unit], start_fill_of[unit]

    assert len(fill_of) == FILLS and FILLS % RING == 0 and PROJECTIONS % RING == 0
    assert all(x[:2] == ("project", V) for x, n in fill_of.items() if n >= FREED)

    ctx = ExitStack()
    with ctx:
        def sb(name, shape, dt, stack=ctx):
            return stack.enter_context(nc.sbuf_tensor(name, shape, dt))

        def sem(name):
            return ctx.enter_context(nc.semaphore(name))

        x_acc = sb("x_acc", [P, NT, D], f32)
        ws_up = sb("ws_up", [P, 2, HS], f32)
        ws_down = sb("ws_down", [P, SB, D], f32)
        wq_sb = sb("wq_sb", [P, HEADS, DH], f32)
        wk_sb = sb("wk_sb", [P, HEADS, DH], f32)
        wv_sb = sb("wv_sb", [P, HEADS * DH], f32)
        wo_sb = sb("wo_sb", [P, PAIRS, D], f32)
        wgate_sb = sb("wgate_sb", [P, HEADS], f32)
        wr_sb = sb("wr_sb", [P, E], f32)
        rmsw = sb("rmsw", [P, 1], f32)
        ident = sb("ident", [P, P], f32)
        zeros = sb("zeros", [P, BANK], f32)
        empty_row = sb("empty_row", [P, SLOT_TILES], i32)
        ident_b = sb("ident_b", [P, P], bf16)
        mask_b = sb("mask_b", [P, P], bf16)
        stat = sb("stat", [P, 4, NT], f32)
        b2_e = sb("b2_e", [E, D], f32)
        b2_r = sb("b2_r", [E, D], f32)
        b2_s = sb("b2_s", [E, 3, D], bf16)
        b2_rows = sb("b2_rows", [3, E * D], bf16)
        b_col = sb("b_col", [P, E, UP // P], f32)
        bs_col = sb("bs_col", [P, 2, SB], f32)
        bs2_all = sb("bs2_all", [P, D], f32)
        ones3 = sb("ones3", [3, P], bf16)
        ones_b = sb("ones_b", [P, P], bf16)
        tri_b = sb("tri_b", [P, P], bf16)
        bn = sb("bn", [P, NT, 6], f32)
        mv = sb("mv", [P, NT, 2], f32)
        rstd = sb("rstd", [P, 2, NT], f32)
        attn = ExitStack()
        tT = sb("tT", [P, N], f32, attn)
        q_hl = [sb(f"q_hl{h}", [P, N], f32r, attn) for h in range(2)]
        k_h = [sb(f"k_h{h}", [P, N], f32r, attn) for h in range(2)]
        k_l = [sb(f"k_l{h}", [P, N], f32r, attn) for h in range(2)]
        v_sb = sb("v_sb", [P, NT, P], f32, attn)
        probs = [[sb(f"probs{b}{h}", [P, N], f32, attn) for h in range(2)] for b in range(2)]
        xn = probs[0][0][:, :].rearrange("p (n d) -> p n d", d=D)
        probsT = [[sb(f"probsT{b}{h}", [P, NT, P], f32, attn) for h in range(2)] for b in range(2)]
        wkq_p = sb("wkq_p", [P, 2, P], f32, attn)
        wo_p = sb("wo_p", [P, D], f32, attn)
        outT = [[sb(f"outT{b}{h}", [P, P], f32, attn) for h in range(2)] for b in range(2)]
        gate1 = sb("gate1", [P, NT, HEADS], f32, attn)
        cmax = sb("cmax", [P, 2, NC], f32, attn)
        nmax = sb("nmax", [P, 2 * NT], f32, attn)
        rsum = sb("rsum", [P, 2 * NT], f32, attn)
        rden = sb("rden", [P, 2, 2], f32, attn)
        attn.close()
        moe = ExitStack()
        xT = sb("xT", [P, N], f32, moe)
        w_up = sb("w_up", [P, E, UP], f32, moe)
        w_down = sb("w_down", [P, E, HB, D], f32, moe)
        rows = sb("rows", [P, TOPK, NT, D + 1], f32, moe)
        logits = sb("logits", [P, NT, E], f32, moe)
        top8 = sb("top8", [P, NT, 8], f32, moe)
        idx8 = sb("idx8", [P, NT, 8], u32, moe)
        shared = sb("shared", [P, NT, D], f32, moe)
        idxf = sb("idxf", [P, TOPK, NT], f32, moe)
        ie = sb("ie", [P, NT, E], f32, moe)
        hot = sb("hot", [P, TOPK, NT, E], f32, moe)
        routed = sb("routed", [P, NT * E], bf16, moe)
        rank = sb("rank", [P, NT, E], f32, moe)
        counts = sb("counts", [P, E * NT + 1], f32, moe)
        before = sb("before", [P, E * NT + 1], f32, moe)
        cnt_i = sb("cnt_i", [P, E], i32, moe)
        tiles_n = sb("tiles_n", [P, E], f32, moe)
        tiles_end = sb("tiles_end", [P, E], f32, moe)
        ones_row = sb("ones_row", [P, E * NT + 1], f32, moe)
        base = sb("base", [P, E], f32, moe)
        picked = sb("picked", [P, TOPK, NT, E], f32, moe)
        slot_f = sb("slot_f", [P, TOPK, NT], f32, moe)
        slot = sb("slot", [P, TOPK, NT], u32, moe)
        it = sb("it", [1, ROUNDS, IDS, E], f32, moe)
        past = sb("past", [1, ROUNDS * IDS, E], f32, moe)
        exp_f = sb("exp_f", [1, ROUNDS * IDS], f32, moe)
        exp_i = sb("exp_i", [1, ROUNDS * IDS], i32, moe)
        gat = sb("gat", [P, 4, NT], f32, moe)
        sil_s = sb("sil_s", [P, 2, BANK], f32, moe)
        act_s = sb("act_s", [P, 2, SB, BANK], f32, moe)
        w_now = sb("w_now", [P, 2, UP + HB], f32, moe)
        xg = sb("xg", [P, ROUND, D + 1], f32, moe)
        row_all = sb("row_all", [P, SLOT_TILES], i32, moe)
        row_now = sb("row_now", [P, 2], u32, moe)
        xgT = sb("xgT", [P, 2, P], f32, moe)
        sil = sb("sil", [P, 2, H], f32, moe)
        hid = sb("hid", [P, 2, H], f32, moe)
        y_sb = sb("y_sb", [P, 2, D], f32, moe)
        yg = act_s[:, :, :, :].rearrange("p k m (j d) -> p k (m j) d", d=D)
        moe.close()

        x_sorted = nc.dram_tensor("x_sorted", (SLOTS, D + 1), f32, kind="Internal").ap()
        y_rows = nc.dram_tensor("y_rows", (TOPK * N + SLOTS, D), f32, kind="Internal").ap()

        def bank(name):
            return ctx.enter_context(nc.psum_tensor(name, [P, BANK], f32))

        ps_s = [bank(f"ps_s{i}") for i in range(RING)]
        ps_t = [bank(f"ps_t{i}") for i in range(2)]
        ps_o = [bank(f"ps_o{i}") for i in range(2)]

        def up_bank(n, a):
            return ((ps_s[1], ps_s[2]), (ps_s[3], ps_o[1]))[n % 2][a]

        def logit_bank(c):
            return ps_t[1] if c == n3 else ps_s[0]

        def x_bank(i):
            return ps_t[0] if i == NC - 1 else ps_s[NC - 1 - i]

        x_in = [sem(f"x_in{c}") for c in range(NC)]
        start_w, w_in, wo_in, gw_in = sem("start_w"), sem("w_in"), sem("wo_in"), sem("gw_in")
        moe_in, shw_in, bias_in, brow_in = sem("moe_in"), sem("shw_in"), sem("bias_in"), sem("brow_in")
        out_done = sem("out_done")
        zero_set, zfill, consts, ident_set = sem("zero_set"), sem("zfill"), sem("consts"), sem("ident_set")
        pool_step = sem("pool_step")
        dve_step, act_step = sem("dve_step"), sem("act_step")
        bias_split, bcol_in = sem("bias_split"), sem("bcol_in")
        ms_ready, std_ready, rms_ready, xn_ready, xnT_ready, tT_ready = (sem(n) for n in (
            "ms_ready", "std_ready", "rms_ready", "xn_ready", "xnT_ready", "tT_ready"))
        z_ready, ez_ready, gate_ready = sem("z_ready"), sem("ez_ready"), sem("gate_ready")
        pair_w, pair_wo, k_twice, v_ready = (sem(n) for n in ("pair_w", "pair_wo", "k_twice", "v_ready"))
        fill, freed, high = sem("fill"), sem("freed"), sem("high")
        row_max, exp_done = sem("row_max"), sem("exp_done")
        turned, moved0, moved1 = sem("turned"), sem("moved0"), sem("moved1")
        pv_done, out_ready, wo_done, acc_done = sem("pv_done"), sem("out_ready"), sem("wo_done"), sem("acc_done")
        loop_step = sem("loop_step")
        var_ready, ln_std, x1_ready = sem("var_ready"), sem("ln_std"), sem("x1_ready")
        x1T_psum, x1T_ready = sem("x1T_psum"), sem("x1T_ready")
        lg_psum, gexp = sem("lg_psum"), sem("gexp")
        routed_ready, count_psum, slots_ready, expert_ready = (sem(n) for n in (
            "routed_ready", "count_psum", "slots_ready", "expert_ready"))
        scattered, rows_ready = sem("scattered"), sem("rows_ready")
        shared_set = sem("shared_set")
        row_noted, row_set, sent = sem("row_noted"), sem("row_set"), sem("sent")
        yg_in = [sem(f"yg_in{c}") for c in range(NC)]
        up_s, sil_done, act_done, down_s, shared_done = (sem(n) for n in (
            "up_s", "sil_done", "act_done", "down_s", "shared_done"))
        xg_in = [sem(f"xg_in{b}") for b in range(ROUND)]
        w_ready = sem("w_ready")
        y_out = [sem(f"y_out{b}") for b in range(2)]
        xgT_psum, xgT_ready, up_e, sil_e, hid_e = (sem(n) for n in (
            "xgT_psum", "xgT_ready", "up_e", "sil_e", "hid_e"))
        down_e, y_ready = sem("down_e"), sem("y_ready")
        fin_var, fin_std, fin_ready = sem("fin_var"), sem("fin_std"), sem("fin_ready")

        def by_dma(n, b, buffers):
            return (n + (buffers - b)) * (16 // buffers)

        def expert_slots(engine, slot):
            slot(0, -1, up=False, down=False)
            slot(0, 0, down=False)
            for j in range(1, ROUND):
                slot(0, j)
            with engine.Fori(1, ROUNDS - 2) as r:
                for j in range(ROUND):
                    slot(r, j)
            for j in range(ROUND):
                slot(ROUNDS - 2, j, next=j < ROUND - 1)
            slot(ROUNDS - 1, 0, up=False, next=False)

        ONE = 1

        block = ctx.enter_context(nc.Block())

        @block.sync
        def _(sp):
            for s in (wo_done, pv_done, turned, freed, moved0, moved1, out_ready, acc_done):
                sp.sem_inc(s, ONE)
            for c in range(NC):
                sp.dma_start(x_acc[:, c * BT:(c + 1) * BT, :],
                             tokens[0, c * BANK:(c + 1) * BANK, :].rearrange("(n p) d -> p n d", p=P)).then_inc(x_in[c], 16)
            sp.dma_start(rmsw[:, :], rms_w.rearrange("(p a) -> p a", a=1)).then_inc(gw_in, 16)
            sp.dma_start(wgate_sb[:, :], w_gates).then_inc(gw_in, 16)
            sp.dma_start(wr_sb[:, :], Wg).then_inc(gw_in, 16)
            for w, src in ((K, wk), (Q, wq)):
                sp.dma_start(wkq_p[:, w, :].rearrange("d (a e) -> d a e", a=2),
                             src[0:2].rearrange("h d e -> d h e")).then_inc(start_w, 16)
            sp.dma_start(wq_sb[:, :, :], wq.rearrange("h d e -> d h e")).then_inc(w_in, 16)
            sp.dma_start(wk_sb[:, :, :], wk.rearrange("h d e -> d h e")).then_inc(w_in, 16)
            sp.dma_start(wv_sb[:, :].rearrange("d (h e) -> d h e", h=HEADS),
                         wv.rearrange("h d e -> d h e")).then_inc(w_in, 16)
            sp.dma_start(wo_sb[:, :, :], wo.rearrange("(n a) e d -> (a e) n d", a=2)).then_inc(wo_in, 16)
            sp.dma_start(b2_e[:, :], b2).then_inc(bias_in, 16)
            with nc.allow_non_contiguous_dma("a column of biases on each partition, 1 KB"):
                sp.dma_start(bs_col[:, 0, :], bs1.rearrange("(m p) -> p m", p=P)).then_inc(shw_in, 16)
                sp.dma_start(bs_col[:, 1, :], bs11.rearrange("(m p) -> p m", p=P)).then_inc(shw_in, 16)
            sp.dma_start(bs2_all[:, :], bs2.rearrange("(a d) -> a d", a=1).to_broadcast([P, D])).then_inc(shw_in, 16)
            sp.dma_start(ws_up[:, 0, :], Ws1).then_inc(shw_in, 16)
            sp.dma_start(ws_up[:, 1, :], Ws11).then_inc(shw_in, 16)
            sp.dma_start(ws_down[:, :, :], Ws2.rearrange("(m p) d -> p m d", p=P)).then_inc(shw_in, 16)
            def k_across(unit, highs, frees):
                c = unit[3]
                cols = slice(c * BANK, (c + 1) * BANK)
                for k_part, part_ready, count in ((k_h, high, highs + 1), (k_l, freed, frees + 1)):
                    sp.wait_ge(part_ready, count)
                    for h in range(2):
                        rows, other = slice(h * DH, (h + 1) * DH), slice((1 - h) * DH, (2 - h) * DH)
                        sp.dma_start(k_part[h][other, cols].bitcast(f32),
                                     k_part[h][rows, cols].bitcast(f32)).then_inc(k_twice, 16)

            for x in START:
                if x[1] == K:
                    k_across(x, start_high_of[x], start_fill_of[x] + ONE)
            with sp.Fori(0, PAIRS - 1) as p:
                for x in MORE:
                    if x[:2] == ("project", K):
                        k_across(x, p * KQ_FILLS + (KQ_FILLS + high_of[x]),
                                 p * FREED + (KQ_FILLS + fill_of[x] + ONE))
            sp.wait_ge(zero_set, 2)
            view = x_sorted.rearrange("(g n p) d -> g p n d", p=P, n=BT)
            for g in range(SLOT_TILES // BT):
                sp.dma_start(view[g, :, :, 0:D], zeros[:, :].rearrange("p (n d) -> p n d", d=D)).then_inc(zfill, 16)
            with nc.allow_non_contiguous_dma("one number of each row, 24 KB"):
                sp.dma_start(x_sorted.rearrange("(n p) d -> p n d", p=P)[:, :, D].bitcast(i32),
                             empty_row[:, :]).then_inc(zfill, 16)
            with nc.allow_non_contiguous_dma("a column of biases of each block of hidden values, 16 KB"):
                for a, b in enumerate((b1, b11)):
                    for e in range(E):
                        sp.dma_start(b_col[:, e, a * HB:(a + 1) * HB],
                                     b[e].rearrange("(m p) -> p m", p=P)).then_inc(bcol_in, 16)
            sp.wait_ge(bias_split, 5)
            for k in range(3):
                sp.dma_start(b2_rows[k:k + 1, :].rearrange("a (e n) -> a e n", e=E),
                             b2_s[:, k, :]).then_inc(brow_in, 16)
            sp.wait_ge(freed, ONE + KQ_FILLS + (PAIRS - 1) * FREED + GROUPS)
            sp.dma_start(w_up[:, :, 0:H], W1.rearrange("e d h -> d e h")).then_inc(moe_in, 16)
            sp.dma_start(w_up[:, :, H:UP], W11.rearrange("e d h -> d e h")).then_inc(moe_in, 16)
            sp.dma_start(w_down[:, :, :, :], W2.rearrange("e (m p) d -> p e m d", p=P)).then_inc(moe_in, 16)
            sp.wait_ge(scattered, 16 * TOPK * NT)
            for b in range(ROUND):
                sp.dma_start(xg[:, b, :], x_sorted[b * P:(b + 1) * P, :]).then_inc(xg_in[b], 16)
            with sp.Fori(1, SLOT_TILES // ROUND) as r:
                for b in range(ROUND):
                    sp.wait_ge(xgT_psum, r * ROUND + (b + 1 - ROUND))
                    sp.wait_ge(row_noted, r * ROUND + (b + 1 - ROUND))
                    sp.dma_start(xg[:, b, :], x_sorted[bass.ds(r * (ROUND * P) + b * P, P), :]).then_inc(xg_in[b], 16)
            for b in range(2):
                sp.wait_ge(y_out[b], 16 * (SLOT_TILES // 2))
            for c in range(NC):
                for k in range(TOPK):
                    at = k * N + c * BANK
                    sp.dma_start(yg[:, k, c * BT:(c + 1) * BT, :],
                                 y_rows[at:at + BANK, :].rearrange("(n p) d -> p n d", p=P)).then_inc(yg_in[c], 16)
            for c in range(NC):
                sp.wait_ge(fin_ready, BT * (c + 1))
                sp.dma_start(out[0, c * BANK:(c + 1) * BANK, :].rearrange("(n p) d -> p n d", p=P),
                             x_acc[:, c * BT:(c + 1) * BT, :]).then_inc(out_done, 16)
            sp.wait_ge(out_done, 16 * NC)

        @block.gpsimd
        def _(pool):
            nc.gpsimd.memset(ident[:, :], 0.0).then_inc(pool_step, 1)
            nc.gpsimd.memset(mask_b[:, :], 0.0).then_inc(pool_step, 1)
            nc.gpsimd.memset(tri_b[:, :], 1.0).then_inc(pool_step, 1)
            nc.gpsimd.memset(ones_b[:, :], 1.0).then_inc(consts, 1)
            nc.gpsimd.memset(ones3[:, :], 1.0).then_inc(consts, 1)
            nc.gpsimd.memset(zeros[:, :], 0.0).then_inc(zero_set, 1)
            for b in range(2):
                for h in range(2):
                    nc.gpsimd.memset(outT[b][h][:, :], 0.0).then_inc(consts, 1)
            nc.gpsimd.memset(ident_b[:, :], 0.0).then_inc(pool_step, 1)
            nc.gpsimd.iota(empty_row[:, :], pattern=[[P, SLOT_TILES]], base=TOPK * N,
                           channel_multiplier=1).then_inc(zero_set, 1)
            pool.wait_ge(pool_step, 4)
            nc.gpsimd.affine_select(out=ident[:, :], in_=ident[:, :], compare_op=ALU.not_equal, fill=1.0,
                                    base=0, pattern=[[-1, P]], channel_multiplier=1).then_inc(ident_set, 1)
            nc.gpsimd.affine_select(out=ident_b[:, :], in_=ident_b[:, :], compare_op=ALU.not_equal, fill=1.0,
                                    base=0, pattern=[[-1, P]], channel_multiplier=1).then_inc(ident_set, 1)
            nc.gpsimd.affine_select(out=mask_b[:, :], in_=mask_b[:, :], compare_op=ALU.is_ge,
                                    fill=MASKED, base=0, pattern=[[-1, P]], channel_multiplier=1).then_inc(consts, 1)
            nc.gpsimd.affine_select(out=tri_b[:, :], in_=tri_b[:, :], compare_op=ALU.is_gt, fill=0.0,
                                    base=0, pattern=[[1, P]], channel_multiplier=-1).then_inc(consts, 1)
            pool.wait_ge(w_in, 48)
            pool.wait_ge(wo_in, 16)
            def project_weights(p):
                for n, w in enumerate((wk_sb, wq_sb)):
                    nc.gpsimd.tensor_copy(wkq_p[:, n, :].rearrange("d (a e) -> d a e", a=2),
                                          w[:, bass.ds(p * 2, 2), :]).then_inc(pair_w, 1)

            def out_weights(p):
                nc.gpsimd.tensor_copy(wo_p[:, :], wo_sb[:, bass.ds(p, 1), :]
                                      .rearrange("d a e -> d (a e)")).then_inc(pair_wo, 1)

            out_weights(0)
            pool.wait_ge(bias_in, 16)
            splits = [0]

            def split(ins):
                splits[0] += 1
                ins.then_inc(bias_split, 1)
                pool.wait_ge(bias_split, splits[0])

            split(nc.gpsimd.tensor_copy(b2_s[:, 0, :], b2_e[:, :]))
            split(nc.gpsimd.tensor_tensor(b2_r[:, :], b2_e[:, :], b2_s[:, 0, :], ALU.subtract))
            split(nc.gpsimd.tensor_copy(b2_s[:, 1, :], b2_r[:, :]))
            split(nc.gpsimd.tensor_tensor(b2_e[:, :], b2_r[:, :], b2_s[:, 1, :], ALU.subtract))
            split(nc.gpsimd.tensor_copy(b2_s[:, 2, :], b2_e[:, :]))
            with pool.Fori(1, PAIRS) as p:
                pool.wait_ge(fill, (p - 1) * FILLS + PROJECTIONS)
                project_weights(p)
                pool.wait_ge(wo_done, p * NT + ONE)
                out_weights(p)
            pool.wait_ge(acc_done, ONE + PAIRS * NT)
            nc.gpsimd.iota(ie[:, :, :], pattern=[[0, NT], [1, E]], base=0, channel_multiplier=0,
                           allow_small_or_imprecise_dtypes=True).then_inc(pool_step, 1)
            nc.gpsimd.iota(it[:, :, :, :], pattern=[[ROUND, ROUNDS], [1, IDS], [0, E]], base=-2, channel_multiplier=0,
                           allow_small_or_imprecise_dtypes=True).then_inc(pool_step, 1)
            nc.gpsimd.iota(rows[:, :, :, D].bitcast(i32), pattern=[[N, TOPK], [P, NT]], base=0,
                           channel_multiplier=1).then_inc(pool_step, 1)
            nc.gpsimd.memset(counts[:, 0:1], 0.0).then_inc(pool_step, 1)
            nc.gpsimd.memset(ones_row[:, :], 1.0).then_inc(pool_step, 1)
            pool.wait_ge(shw_in, 16 * 6)
            for i, c in enumerate(NORM_ORDER):
                cols = slice(c * BT, (c + 1) * BT)
                pool.wait_ge(x1_ready, BT * (i + 1))
                nc.gpsimd.tensor_tensor(shared[:, cols, :], rows[:, 0, cols, 0:D],
                                        bs2_all[:, :].unsqueeze(1).to_broadcast([P, BT, D]), ALU.add).then_inc(shared_set, 1)
            pool.wait_ge(pool_step, 9)
            pool.wait_ge(zfill, 16 * (SLOT_TILES // BT + 1))
            pool.wait_ge(rows_ready, NC)
            pool.wait_ge(slots_ready, 1)
            for t in range(NT):
                for k in range(TOPK):
                    nc.gpsimd.indirect_dma_start(
                        out=x_sorted, out_offset=bass.IndirectOffsetOnAxis(ap=slot[:, k, t:t + 1], axis=0),
                        in_=rows[:, k, t, :], in_offset=None).then_inc(scattered, 16)
            def send(n, b):
                pool.wait_ge(row_noted, n + 1)
                nc.gpsimd.tensor_copy(row_now[:, b:b + 1], row_all[:, bass.ds(n, 1)]).then_inc(row_set, 1)
                pool.wait_ge(row_set, n + 1)
                pool.wait_ge(y_ready, n + 1)
                pool.sem_inc(sent, 1)
                nc.gpsimd.indirect_dma_start(
                    out=y_rows, out_offset=bass.IndirectOffsetOnAxis(ap=row_now[:, b:b + 1], axis=0),
                    in_=y_sb[:, b, :], in_offset=None).then_inc(y_out[b], 16)

            for b in range(2):
                send(b, b)
            with pool.Fori(1, SLOT_TILES // 2) as i:
                for b in range(2):
                    pool.wait_ge(y_out[b], i * 16)
                    send(i * 2 + b, b)

        @block.scalar
        def _(act):
            def project(unit, n, fills, p):
                _, w, _, c, _ = unit
                act.wait_ge(fill, fills + 1)
                if w == V:
                    if p is not None:
                        act.wait_ge(pv_done, p * NT + (ONE + last_use[c] + 1))
                    nc.scalar.activation(v_sb[:, c * BT:(c + 1) * BT, :].rearrange("p n e -> p (n e)"),
                                         ps_s[n % RING][:, :], ACT.Copy).then_inc(v_ready, 1)
                else:
                    for h in range(2):
                        rows = slice(h * DH, (h + 1) * DH)
                        ins = nc.scalar.activation((k_h, q_hl)[w][h][rows, c * BANK:(c + 1) * BANK],
                                                   ps_s[n % RING][rows, :], ACT.Copy)
                    ins.then_inc(high, 1)

            for i in range(NC + 2):
                if i < NC:
                    cols = slice(i * BT, (i + 1) * BT)
                    act.wait_ge(ms_ready, i + 1)
                    nc.scalar.activation(stat[:, 1, cols], stat[:, 0, cols], ACT.Sqrt).then_inc(std_ready, 1)
                    act.wait_ge(rms_ready, i + 1)
                    for t in range(i * BT, (i + 1) * BT):
                        ins = nc.scalar.activation(xn[:, t, :], x_acc[:, t, :], ACT.Copy, scale=stat[:, 2, t:t + 1])
                    ins.then_inc(xn_ready, 1)
                if i >= 2:
                    for w in (K, Q):
                        project(*started("project", w, 0, i - 2, 0), None)
            act.wait_ge(z_ready, 1)
            nc.scalar.activation(gate1[:, :, :].rearrange("p n h -> p (n h)"), ps_o[0][:, 0:NT * HEADS], ACT.Exp,
                                 scale=-1.0).then_inc(ez_ready, 1)
            for c in range(NC):
                project(*started("project", V, 0, c, 0), None)
            def norm(stage, c):
                i, cols = NORM_ORDER.index(c), slice(c * BT, (c + 1) * BT)
                if stage == "stats":
                    act.wait_ge(var_ready, i + 1)
                    nc.scalar.activation(rstd[:, 0, cols], rstd[:, 1, cols], ACT.Sqrt).then_inc(ln_std, 1)
                elif stage == "turn_x":
                    act.wait_ge(x1T_psum, i + 1)
                    nc.scalar.activation(xT[:, c * BANK:(c + 1) * BANK], x_bank(i)[:, :], ACT.Copy).then_inc(x1T_ready, 1)
                else:
                    act.wait_ge(x1_ready, BT * (i + 1))
                    nc.scalar.activation(rows[:, 1, cols, 0:D], rows[:, 0, cols, 0:D], ACT.Copy).then_inc(rows_ready, 1)

            with act.Fori(0, PAIRS) as p:
                def exps(s, h):
                    w = (ORDER[s] + 1) * P
                    row = slice(2 * s + h, 2 * s + h + 1)
                    act.wait_ge(row_max, p * (2 * NT) + (2 * s + h + 1))
                    nc.scalar.activation(probs[s % 2][h][:, 0:w], probs[s % 2][h][:, 0:w], ACT.Exp,
                                         bias=nmax[:, row], scale=SCALE,
                                         accum_out=rsum[:, row]).then_inc(exp_done, 1)

                def move(s, h, c, w):
                    g = first[s, h] + c
                    if g % 2 == 0:
                        if s >= 2:
                            act.wait_ge(pv_done, p * NT + (ONE + s - 1))
                        act.wait_ge(turned, p * GROUPS + (ONE + g + 1))
                        nc.scalar.activation(
                            probsT[s % 2][h][:, c * BT:c * BT + w // P, :].rearrange("p n i -> p (n i)"),
                            ps_t[0][:, 0:w], ACT.Copy).then_inc(moved0, 1)

                def unload(s):
                    act.wait_ge(pv_done, p * NT + (ONE + s + 1))
                    act.wait_ge(wo_done, p * NT + (ONE + max(s - 1, 0)))
                    for h in range(2):
                        rows = slice(h * DH, (h + 1) * DH)
                        nc.scalar.activation(outT[s % 2][h][rows, :], ps_o[s % 2][rows, 0:P], ACT.Copy).then_inc(out_ready, 1)

                def run(units, fill_of):
                    for x in units:
                        stage, s, h, c, w = x
                        if stage == "project":
                            project(x, fill_of[x], p * FILLS + (PROJECTIONS + fill_of[x]), p)
                        elif stage == "scores" and (c, w) == chunks[s][-1]:
                            exps(s, h)
                        elif stage == "turn":
                            move(s, h, c, w)
                        elif stage == "times_v" and (c, w) == chunks[s][-1]:
                            unload(s)
                        elif stage in ("stats", "norm", "turn_x"):
                            norm(stage, c)

                run(HEAD, fill_of)
                with act.If(p < PAIRS - 1):
                    run(MORE, fill_of)
                with act.Else():
                    run(LAST, last_fill_of)

            norm("stats", n3)
            norm("turn_x", n2)
            norm("turn_x", n3)
            norm("norm", n2)
            norm("norm", n3)
            act.wait_ge(shw_in, 16 * 6)
            act.wait_ge(acc_done, ONE + PAIRS * NT)
            for n in range(NC * SB):
                m = n % SB
                act.wait_ge(up_s, n + 1)
                if n >= 2:
                    act.wait_ge(act_done, n - 1)
                nc.scalar.activation(sil_s[:, n % 2, :], up_bank(n, 0)[:, :], ACT.Silu,
                                     bias=bs_col[:, 0, m:m + 1]).then_inc(sil_done, 1)
            def expert_slot(r, j, up=True, next=True, down=True):
                n, b, o = r * ROUND + j, j % 2, 1 - j % 2
                if next:
                    act.wait_ge(xgT_psum, n + 2)
                    nc.scalar.activation(xgT[:, o, :], ps_t[o][:, 0:P], ACT.Copy).then_inc(xgT_ready, 1)
                if up:
                    act.wait_ge(up_e, n * 2 + 1)
                    for m in range(HB):
                        cols = slice(m * P, (m + 1) * P)
                        nc.scalar.activation(sil[:, b, cols], ps_s[2 * b][:, cols], ACT.Silu,
                                             bias=w_now[:, b, UP + m:UP + m + 1]).then_inc(sil_e, 1)
                if down:
                    if not isinstance(n, int) or n >= 3:
                        act.wait_ge(y_out[o], by_dma(n - 3, o, 2))
                    act.wait_ge(down_e, n)
                    nc.scalar.activation(y_sb[:, o, :], ps_o[o][:, 0:D], ACT.Copy).then_inc(y_ready, 1)

            expert_slots(act, expert_slot)
            act.wait_ge(gexp, 1)
            nc.scalar.activation(gat[:, 1, :], gat[:, 0, :], ACT.Exp).then_inc(gexp, 1)
            for c in range(NC):
                cols = slice(c * BT, (c + 1) * BT)
                act.wait_ge(fin_var, c + 1)
                nc.scalar.activation(rstd[:, 0, cols], rstd[:, 1, cols], ACT.Sqrt).then_inc(fin_std, 1)

        @block.vector
        def _(dve):
            steps = [0]

            def link(ins):
                steps[0] += 1
                ins.then_inc(dve_step, 1)
                dve.wait_ge(dve_step, steps[0])

            def project(unit, n, highs):
                _, w, _, c, _ = unit
                if w != V:
                    dve.wait_ge(high, highs + 1)
                    cols = slice(c * BANK, (c + 1) * BANK)
                    for h in range(2):
                        rows = slice(h * DH, (h + 1) * DH)
                        free = slice((1 - h) * DH, (2 - h) * DH)
                        low = (k_l[h][rows, cols], q_hl[h][free, cols])[w]
                        ins = nc.vector.tensor_tensor(low, ps_s[n % RING][rows, :],
                                                      (k_h, q_hl)[w][h][rows, cols].bitcast(f32), ALU.subtract)
                    ins.then_inc(freed, 1)

            for i in range(NC + 2):
                if i < NC:
                    cols = slice(i * BT, (i + 1) * BT)
                    dve.wait_ge(x_in[i], 16)
                    for t in range(i * BT, (i + 1) * BT):
                        ins = nc.vector.tensor_tensor_reduce(out=xn[:, t, :], in0=x_acc[:, t, :], in1=x_acc[:, t, :],
                                                             scale=1.0 / D, scalar=RMS_EPS, op0=ALU.mult, op1=ALU.add,
                                                             accum_out=stat[:, 0, t:t + 1])
                    ins.then_inc(ms_ready, 1)
                    dve.wait_ge(std_ready, i + 1)
                    nc.vector.reciprocal(stat[:, 2, cols], stat[:, 1, cols]).then_inc(rms_ready, 1)
                if i == 0:
                    dve.wait_ge(gw_in, 48)
                if 1 <= i <= NC:
                    c = i - 1
                    dve.wait_ge(xnT_ready, c + 1)
                    nc.vector.tensor_scalar(tT[:, c * BANK:(c + 1) * BANK], ps_t[c % 2][:, :], rmsw[:, 0:1], None,
                                            ALU.mult).then_inc(tT_ready, 1)
                if i >= 2:
                    for w in (K, Q):
                        x = ("project", w, 0, i - 2, 0)
                        project(x, start_fill_of[x], start_high_of[x])
            dve.wait_ge(ez_ready, 1)
            nc.vector.tensor_scalar(gate1[:, :, :], gate1[:, :, :], 1.0, None, ALU.add).then_inc(gate_ready, 1)
            dve.wait_ge(gate_ready, 1)
            dve.wait_ge(consts, 8)
            def statistics(src, tiles):
                for t in tiles:
                    ins = nc.vector.bn_stats(bn[:, t, :], src(t))
                link(ins)
                for t in tiles:
                    ins = nc.vector.bn_aggr(mv[:, t, :], bn[:, t, :])
                link(ins)

            def norm(stage, c):
                i, tiles, cols = NORM_ORDER.index(c), range(c * BT, (c + 1) * BT), slice(c * BT, (c + 1) * BT)
                if stage == "stats":
                    dve.wait_ge(acc_done, (PAIRS - 1) * NT + ONE + summed[c])
                    statistics(lambda t: x_acc[:, t, :], tiles)
                    nc.vector.tensor_scalar(rstd[:, 1, cols], mv[:, cols, 1], LN_EPS, None, ALU.add).then_inc(var_ready, 1)
                else:
                    dve.wait_ge(ln_std, i + 1)
                    link(nc.vector.reciprocal(rstd[:, 1, cols], rstd[:, 0, cols]))
                    for t in tiles:
                        nc.vector.tensor_scalar(rows[:, 0, t, 0:D], x_acc[:, t, :], mv[:, t, 0:1], rstd[:, 1, t:t + 1],
                                                ALU.subtract, ALU.mult).then_inc(x1_ready, 1)

            def largest_logits(chunks, bank):
                tiles = range(min(chunks) * BT, (max(chunks) + 1) * BT)
                cols = slice(tiles[0], tiles[-1] + 1)
                dve.wait_ge(lg_psum, NORM_ORDER.index(chunks[-1]) + 1)
                link(nc.vector.tensor_copy(logits[:, cols, :].rearrange("p n e -> p (n e)"),
                                           bank[:, tiles[0] * E:(tiles[-1] + 1) * E]))
                for t in tiles:
                    ins = nc.vector.max(top8[:, t, :], logits[:, t, :])
                link(ins)
                for t in tiles:
                    ins = nc.vector.max_index(idx8[:, t, :], top8[:, t, :], logits[:, t, :])
                link(ins)

            LINKS = 5 * NT
            with dve.Fori(0, PAIRS) as p:
                count = [0]

                def link_in(ins):
                    count[0] += 1
                    ins.then_inc(loop_step, 1)
                    dve.wait_ge(loop_step, p * LINKS + count[0])

                def scores(s, h, c, w, n):
                    if c == 0 and s >= 2:
                        dve.wait_ge(turned, p * GROUPS + (ONE + group_end(s - 2, h)))
                    dve.wait_ge(fill, p * FILLS + (PROJECTIONS + n + 1))
                    nc.vector.tensor_scalar(
                        probs[s % 2][h][:, c * BANK:c * BANK + w], ps_s[n % RING][:, 0:w], 1.0, None,
                        ALU.mult, ALU.max, accum_out=cmax[:, h, c:c + 1]).then_inc(freed, 1)
                    if c == len(chunks[s]) - 1:
                        row = slice(2 * s + h, 2 * s + h + 1)
                        dve.wait_ge(freed, p * FREED + (KQ_FILLS + n + 1 + ONE))
                        link_in(nc.vector.tensor_reduce(nmax[:, row], cmax[:, h, 0:c + 1], X, ALU.max, negate=True))
                        nc.vector.tensor_scalar(nmax[:, row], nmax[:, row], SCALE, None, ALU.mult).then_inc(row_max, 1)

                def move(s, h, c, w):
                    g = first[s, h] + c
                    if g % 2 == 1:
                        if s >= 2:
                            dve.wait_ge(pv_done, p * NT + (ONE + s - 1))
                        dve.wait_ge(turned, p * GROUPS + (ONE + g + 1))
                        nc.vector.tensor_copy(
                            probsT[s % 2][h][:, c * BT:c * BT + w // P, :].rearrange("p n i -> p (n i)"),
                            ps_t[1][:, 0:w]).then_inc(moved1, 1)

                def add(s):
                    t = ORDER[s]
                    dve.wait_ge(exp_done, p * (2 * NT) + (2 * s + 2))
                    r = rden[:, s % 2, :]
                    link_in(nc.vector.tensor_tensor(r, rsum[:, 2 * s:2 * s + 2],
                                                    gate1[:, t, bass.ds(p * 2, 2)], ALU.mult))
                    link_in(nc.vector.reciprocal(r, r))
                    dve.wait_ge(wo_done, p * NT + (ONE + s + 1))
                    link_in(nc.vector.scalar_tensor_tensor(
                        out=x_acc[:, t, :], in0=ps_o[s % 2][:, P:P + D], scalar=rden[:, s % 2, 0:1], in1=x_acc[:, t, :],
                        op0=ALU.mult, op1=ALU.add))
                    nc.vector.scalar_tensor_tensor(
                        out=x_acc[:, t, :], in0=ps_o[s % 2][:, P + D:P + 2 * D], scalar=rden[:, s % 2, 1:2], in1=x_acc[:, t, :],
                        op0=ALU.mult, op1=ALU.add).then_inc(acc_done, 1)

                def run(units, fill_of):
                    for x in units:
                        stage, s, h, c, w = x
                        if stage == "project":
                            project(x, fill_of[x], p * KQ_FILLS + (KQ_FILLS + high_of.get(x, 0)))
                        elif stage == "scores":
                            scores(s, h, c, w, fill_of[x])
                        elif stage == "turn":
                            move(s, h, c, w)
                        elif stage == "times_wo":
                            add(s)
                        elif stage in ("stats", "norm"):
                            norm(stage, c)

                run(HEAD, fill_of)
                links_before = count[0]
                with dve.If(p < PAIRS - 1):
                    run(MORE, fill_of)
                assert count[0] == LINKS
                count[0] = links_before
                with dve.Else():
                    run(LAST, last_fill_of)
                assert count[0] == LINKS

            norm("stats", n3)
            norm("norm", n2)
            norm("norm", n3)
            largest_logits((n0, n1, n2), logit_bank(n2))
            largest_logits((n3,), logit_bank(n3))
            for k in range(TOPK):
                ins = nc.vector.tensor_copy(idxf[:, k, :], idx8[:, :, k])
            link(ins)
            dve.wait_ge(pool_step, 9)
            link(nc.vector.tensor_tensor(hot[:, :, :, :], ie[:, :, :].unsqueeze(1).to_broadcast([P, TOPK, NT, E]),
                                         idxf[:, :, :].unsqueeze(3).to_broadcast([P, TOPK, NT, E]), ALU.is_equal))
            nc.vector.tensor_tensor(routed[:, :].rearrange("p (n e) -> p n e", e=E), hot[:, 0], hot[:, 1],
                                    ALU.add).then_inc(routed_ready, 1)
            nc.vector.tensor_tensor(gat[:, 0, :], top8[:, :, 1], top8[:, :, 0], ALU.subtract).then_inc(gexp, 1)

            def shared_act(n):
                m = n % SB
                dve.wait_ge(sil_done, n + 1)
                if n // SB >= 2 and m == 0:
                    dve.wait_ge(down_s, n // SB - 1)
                nc.vector.scalar_tensor_tensor(out=act_s[:, n // SB % 2, m, :], in0=up_bank(n, 1)[:, :],
                                               scalar=bs_col[:, 1, m:m + 1], in1=sil_s[:, n % 2, :],
                                               op0=ALU.add, op1=ALU.mult).then_inc(act_done, 1)

            dve.wait_ge(count_psum, 1)
            link(nc.vector.tensor_copy(counts[:, 1:].rearrange("p (e n) -> p e n", e=E),
                                       ps_s[0][:, NT * E:2 * NT * E].rearrange("p (n e) -> p e n", e=E)))
            link(nc.vector.tensor_tensor_scan(before[:, :], ones_row[:, :], counts[:, :], 0.0, ALU.mult, ALU.add))
            starts = before[:, 0:E * NT].rearrange("p (e n) -> p e n", e=E)
            ends = before[:, 1:].rearrange("p (e n) -> p e n", e=E)
            link(nc.vector.scalar_tensor_tensor(out=tiles_n[:, :], in0=ends[:, :, NT - 1], scalar=float(P - 1),
                                                in1=starts[:, :, 0], op0=ALU.add, op1=ALU.subtract))
            link(nc.vector.tensor_copy(cnt_i[:, :], tiles_n[:, :]))
            link(nc.vector.tensor_scalar(cnt_i[:, :], cnt_i[:, :], P.bit_length() - 1, None,
                                         ALU.logical_shift_right))
            link(nc.vector.tensor_copy(tiles_n[:, :], cnt_i[:, :]))
            link(nc.vector.tensor_tensor_scan(tiles_end[:, :], ones_row[:, 0:E], tiles_n[:, :], 0.0, ALU.mult, ALU.add))
            shared_act(0)
            link(nc.vector.tensor_tensor(base[:, :], tiles_end[:, :], tiles_n[:, :], ALU.subtract))
            link(nc.vector.scalar_tensor_tensor(out=base[:, :], in0=base[:, :], scalar=float(P), in1=starts[:, :, 0],
                                                op0=ALU.mult, op1=ALU.subtract))
            link(nc.vector.tensor_tensor(rank[:, :, :], ps_s[0][:, 0:NT * E].rearrange("p (n e) -> p n e", e=E),
                                         starts.rearrange("p e n -> p n e"), ALU.add))
            link(nc.vector.tensor_tensor(rank[:, :, :], rank[:, :, :],
                                         base[:, :].unsqueeze(1).to_broadcast([P, NT, E]), ALU.add))
            shared_act(1)
            link(nc.vector.tensor_tensor(picked[:, :, :, :], hot[:, :, :, :],
                                         rank[:, :, :].unsqueeze(1).to_broadcast([P, TOPK, NT, E]), ALU.mult))
            link(nc.vector.tensor_reduce(slot_f[:, :, :], picked[:, :, :, :], X, ALU.add))
            nc.vector.tensor_copy(slot[:, :, :], slot_f[:, :, :]).then_inc(slots_ready, 1)
            dve.wait_ge(shared_set, NC)

            def shared_add(i):
                c = NORM_ORDER[i]
                dve.wait_ge(down_s, i + 1)
                sh = shared[:, c * BT:(c + 1) * BT, :].rearrange("p n d -> p (n d)")
                nc.vector.tensor_tensor(sh, ps_t[i % 2][:, :], sh, ALU.add).then_inc(shared_done, 1)

            for n in range(2, NC * SB):
                shared_act(n)
                if n == 2 * SB - 1:
                    link(nc.vector.tensor_tensor(past[:, :, :], it[:, :, :, :].rearrange("p r n e -> p (r n) e"),
                                                 tiles_end[0:1, :].unsqueeze(1).to_broadcast([1, ROUNDS * IDS, E]),
                                                 ALU.is_ge))
                if n == 2 * SB + 1:
                    link(nc.vector.tensor_reduce(exp_f[:, :], past[:, :, :], X, ALU.add))
                    link(nc.vector.tensor_scalar(exp_f[:, :], exp_f[:, :], float(E - 1), None, ALU.min))
                    nc.vector.tensor_copy(exp_i[:, :], exp_f[:, :]).then_inc(expert_ready, 1)
                if n % SB == SB - 1 and n >= SB:
                    shared_add(n // SB - 1)
            shared_add(NC - 1)
            dve.wait_ge(bcol_in, 16 * 2 * E)
            dve.wait_ge(moe_in, 48)
            regs = [dve.alloc_register(f"expert_up{k}") for k in range(IDS)]
            experts = []

            def load_experts(r):
                dve.load(regs, exp_i[0:1, bass.ds(r * IDS, IDS)])

            dve.wait_ge(expert_ready, 1)
            load_experts(0)

            def expert_slot(r, j, up=True, next=True, down=True):
                n, b, o = r * ROUND + j, j % 2, 1 - j % 2
                if j == -1 or (j == 0 and not (isinstance(r, int) and r == 0)):
                    experts[:] = [dve.snap(reg, min_val=0, max_val=E - 1) for reg in regs[:ROUND + 3]]
                if next:
                    if not isinstance(n, int) or n >= 1:
                        dve.wait_ge(up_e, n * 2)
                    e = experts[j + 3]
                    nc.vector.tensor_copy(w_now[:, o, 0:UP], w_up[:, bass.ds(e, 1), :].rearrange("p a n -> p (a n)"))
                    nc.vector.tensor_copy(w_now[:, o, UP:], b_col[:, bass.ds(e, 1), 0:HB]
                                          .rearrange("p a n -> p (a n)")).then_inc(w_ready, 1)
                    x = (j + 1) % ROUND
                    dve.wait_ge(xg_in[x], by_dma(n + 1, x, ROUND))
                    nc.vector.tensor_copy(row_all[:, bass.ds(n + 1, 1)],
                                          xg[:, x, D:D + 1].bitcast(i32)).then_inc(row_noted, 1)
                if up:
                    dve.wait_ge(up_e, n * 2 + 2)
                    for m in range(HB):
                        dve.wait_ge(sil_e, n * HB + (m + 1))
                        cols = slice(m * P, (m + 1) * P)
                        ins = nc.vector.scalar_tensor_tensor(
                            out=hid[:, b, cols], in0=ps_s[2 * b + 1][:, cols],
                            scalar=b_col[:, bass.ds(experts[j + 2], 1), HB + m], in1=sil[:, b, cols],
                            op0=ALU.add, op1=ALU.mult)
                    ins.then_inc(hid_e, 1)
                    if j == 0:
                        load_experts(r + 1)

            expert_slots(dve, expert_slot)
            dve.wait_ge(gexp, 2)
            link(nc.vector.tensor_scalar(gat[:, 2, :], gat[:, 1, :], 1.0, None, ALU.add))
            link(nc.vector.reciprocal(gat[:, 2, :], gat[:, 2, :]))
            link(nc.vector.tensor_tensor(gat[:, 3, :], gat[:, 1, :], gat[:, 2, :], ALU.mult))
            for c in range(NC):
                dve.wait_ge(yg_in[c], 16 * TOPK)
                tiles = range(c * BT, (c + 1) * BT)
                cols = slice(c * BT, (c + 1) * BT)
                for k in range(TOPK):
                    for t in tiles:
                        ins = nc.vector.scalar_tensor_tensor(out=shared[:, t, :], in0=yg[:, k, t, :],
                                                             scalar=gat[:, 2 + k, t:t + 1], in1=shared[:, t, :],
                                                             op0=ALU.mult, op1=ALU.add)
                    link(ins)
                statistics(lambda t: shared[:, t, :], tiles)
                nc.vector.tensor_scalar(rstd[:, 1, cols], mv[:, cols, 1], LN_EPS, None, ALU.add).then_inc(fin_var, 1)
                dve.wait_ge(fin_std, c + 1)
                link(nc.vector.reciprocal(rstd[:, 1, cols], rstd[:, 0, cols]))
                for t in tiles:
                    nc.vector.tensor_scalar(x_acc[:, t, :], shared[:, t, :], mv[:, t, 0:1], rstd[:, 1, t:t + 1],
                                            ALU.subtract, ALU.mult).then_inc(fin_ready, 1)

        @block.tensor
        def _(pe):
            def turn(dst, src):
                return nc.tensor.transpose(dst, src, ident[:, :])

            def project(unit, n, q):
                _, w, _, c, _ = unit
                if w == V:
                    for j in range(BT):
                        t = c * BT + j
                        mm = nc.tensor.matmul(ps_s[n % RING][:, j * P:(j + 1) * P], tT[:, t * P:(t + 1) * P],
                                              wv_sb[:, bass.ds(q * P, P)], start=True, stop=True)
                else:
                    mm = nc.tensor.matmul(ps_s[n % RING][:, :], wkq_p[:, w, :],
                                          tT[:, c * BANK:(c + 1) * BANK], start=True, stop=True)
                mm.then_inc(fill, 1)

            def project_start(w, c):
                x = ("project", w, 0, c, 0)
                n = start_fill_of[x]
                if n >= RING:
                    pe.wait_ge(freed, ONE + n - RING + 1)
                project(x, n, 0)

            pe.wait_ge(ident_set, 1)
            for i in range(NC + 1):
                if i < NC:
                    pe.wait_ge(xn_ready, i + 1)
                    if i >= 2:
                        pe.wait_ge(tT_ready, i - 1)
                    for j in range(BT):
                        mm = turn(ps_t[i % 2][:, j * P:(j + 1) * P], xn[:, i * BT + j, :])
                    mm.then_inc(xnT_ready, 1)
                if i >= 1:
                    pe.wait_ge(tT_ready, i)
                    if i == 1:
                        pe.wait_ge(start_w, 32)
                        pe.wait_ge(gw_in, 48)
                    project_start(K, i - 1)
                    project_start(Q, i - 1)
                    for t in range((i - 1) * BT, i * BT):
                        mm = nc.tensor.matmul(ps_o[0][:, t * HEADS:(t + 1) * HEADS], tT[:, t * P:(t + 1) * P],
                                              wgate_sb[:, :], start=True, stop=True)
            mm.then_inc(z_ready, 1)
            pe.wait_ge(w_in, 48)
            for c in range(NC):
                project_start(V, c)
            pe.wait_ge(consts, 8)
            pe.wait_ge(ident_set, 2)
            pe.wait_ge(ez_ready, 1)
            def norm(stage, c):
                i = NORM_ORDER.index(c)
                if stage == "turn_x":
                    pe.wait_ge(x1_ready, BT * (i + 1))
                    for j in range(BT):
                        mm = turn(x_bank(i)[:, j * P:(j + 1) * P], rows[:, 0, c * BT + j, 0:D])
                    mm.then_inc(x1T_psum, 1)
                else:
                    pe.wait_ge(x1T_ready, i + 1)
                    for t in range(c * BT, (c + 1) * BT):
                        mm = nc.tensor.matmul(logit_bank(c)[:, t * E:(t + 1) * E], xT[:, t * P:(t + 1) * P], wr_sb[:, :],
                                              start=True, stop=True)
                    mm.then_inc(lg_psum, 1)

            with pe.Fori(0, PAIRS) as p:
                def free_bank(n):
                    if n < RING:
                        pe.wait_ge(v_ready, p * NC + (n + 1))
                    else:
                        pe.wait_ge(freed, p * FREED + (ONE + KQ_FILLS + n - RING + 1))

                def scores(s, h, c, w, n):
                    t = ORDER[s]
                    if s == 0 and h == 0:
                        pe.wait_ge(freed, p * FREED + (ONE + KQ_FILLS))
                        pe.wait_ge(k_twice, p * (64 * NC) + 64 * NC)
                    free_bank(n)
                    q = q_hl[h][:, t * P:(t + 1) * P]
                    nc.tensor.matmul(ps_s[n % RING][:, 0:w], q, k_h[h][:, c * BANK:c * BANK + w],
                                     start=True, stop=False)
                    if c == len(chunks[s]) - 1:
                        nc.tensor.matmul(ps_s[n % RING][:, w - P:w], ident_b[:, :], mask_b[:, :],
                                         start=False, stop=False, skip_group_check=True)
                    nc.tensor.matmul(ps_s[n % RING][:, 0:w], q, k_l[h][:, c * BANK:c * BANK + w],
                                     start=False, stop=True).then_inc(fill, 1)

                def turn_probs(s, h, c, w):
                    g = first[s, h] + c
                    if c == 0:
                        pe.wait_ge(exp_done, p * (2 * NT) + (2 * s + h + 1))
                    pe.wait_ge((moved0, moved1)[g % 2], p * (GROUPS // 2) + (ONE + g // 2))
                    for j in range(w // P):
                        at = c * BANK + j * P
                        mm = turn(ps_t[g % 2][:, j * P:(j + 1) * P], probs[s % 2][h][:, at:at + P])
                    mm.then_inc(turned, 1)

                def times_v(s, c, w):
                    t = ORDER[s]
                    if c == 0:
                        if s == 0:
                            pe.wait_ge(v_ready, p * NC + NC)
                        done = group_end(s, 1)
                        pe.wait_ge(moved0, p * (GROUPS // 2) + (ONE + (done + 1) // 2))
                        pe.wait_ge(moved1, p * (GROUPS // 2) + (ONE + done // 2))
                        pe.wait_ge(acc_done, p * NT + (ONE + max(s - 1, 0)))
                    for j in range(c * BT, c * BT + w // P):
                        for h in range(2):
                            rows = slice(h * DH, (h + 1) * DH)
                            mm = nc.tensor.matmul(ps_o[s % 2][rows, 0:P], v_sb[:, j, rows], probsT[s % 2][h][:, j, :],
                                                  start=(j == 0), stop=(j == t))
                    if j == t:
                        mm.then_inc(pv_done, 1)

                def times_wo(s):
                    pe.wait_ge(out_ready, p * (2 * NT) + (ONE + 2 * s + 2))
                    if s == 0:
                        pe.wait_ge(pair_wo, p + 1)
                    for h in range(2):
                        mm = nc.tensor.matmul(ps_o[s % 2][:, P + h * D:P + (h + 1) * D], outT[s % 2][h][:, :], wo_p[:, :],
                                              start=True, stop=True)
                    mm.then_inc(wo_done, 1)

                def run(units, fill_of):
                    for x in units:
                        stage, s, h, c, w = x
                        if stage == "project":
                            if high_of.get(x) == 0:
                                pe.wait_ge(pair_w, p * 2 + 2)
                            free_bank(fill_of[x])
                            project(x, fill_of[x], (p + 1).with_bounds(max_val=PAIRS - 1))
                        elif stage == "scores":
                            scores(s, h, c, w, fill_of[x])
                        elif stage == "turn":
                            turn_probs(s, h, c, w)
                        elif stage == "times_v":
                            times_v(s, c, w)
                        elif stage == "times_wo":
                            times_wo(s)
                        elif stage == "turn_x":
                            norm(stage, c)

                run(HEAD, fill_of)
                with pe.If(p < PAIRS - 1):
                    run(MORE, fill_of)
                with pe.Else():
                    run(LAST, last_fill_of)

            def shared_up(n):
                c, m = NORM_ORDER[n // SB], n % SB
                if n >= 2:
                    pe.wait_ge(act_done, n - 1)
                for a in range(2):
                    mm = nc.tensor.matmul(up_bank(n, a)[:, :], ws_up[:, a, m * P:(m + 1) * P],
                                          xT[:, c * BANK:(c + 1) * BANK], start=True, stop=True)
                mm.then_inc(up_s, 1)

            def shared_down(i):
                pe.wait_ge(act_done, SB * (i + 1))
                if i >= 2:
                    pe.wait_ge(shared_done, i - 1)
                for j in range(BT):
                    for m in range(SB):
                        mm = nc.tensor.matmul(ps_t[i % 2][:, j * P:(j + 1) * P],
                                              act_s[:, i % 2, m, j * P:(j + 1) * P], ws_down[:, m, :],
                                              start=(m == 0), stop=(m == SB - 1))
                mm.then_inc(down_s, 1)

            norm("logits", n0)
            norm("logits", n1)
            norm("turn_x", n2)
            pe.wait_ge(moved0, ONE + PAIRS * (GROUPS // 2))
            pe.wait_ge(moved1, ONE + PAIRS * (GROUPS // 2))
            norm("turn_x", n3)
            norm("logits", n2)
            norm("logits", n3)
            pe.wait_ge(shw_in, 16 * 6)
            shared_up(0)
            pe.wait_ge(routed_ready, 1)
            nc.tensor.matmul(ps_s[0][:, 0:NT * E], tri_b[:, :], routed[:, :], start=True, stop=True)
            nc.tensor.matmul(ps_s[0][:, NT * E:2 * NT * E], ones_b[:, :], routed[:, :],
                             start=True, stop=True).then_inc(count_psum, 1)
            for n in range(1, NC * SB):
                shared_up(n)
                if n % SB == SB - 1 and n >= SB:
                    shared_down(n // SB - 1)
            shared_down(NC - 1)
            pe.wait_ge(moe_in, 48)
            pe.wait_ge(brow_in, 48)
            pe.wait_ge(expert_ready, 1)
            pe.wait_ge(shared_done, NC)

            regs = [pe.alloc_register(f"expert{k}") for k in range(IDS)]
            experts = []

            def load_experts(r):
                pe.load(regs, exp_i[0:1, bass.ds(r * IDS, IDS)])

            load_experts(0)

            def expert_slot(r, j, up=True, next=True, down=True):
                n, b, o = r * ROUND + j, j % 2, 1 - j % 2
                if j == 0:
                    experts[:] = [pe.snap(reg, min_val=0, max_val=E - 1) for reg in regs[:ROUND + 1]]
                if next:
                    x = (j + 1) % ROUND
                    pe.wait_ge(xg_in[x], by_dma(n + 1, x, ROUND))
                    if not isinstance(n, int) or n >= 1:
                        pe.wait_ge(xgT_ready, n)
                    turn(ps_t[o][:, 0:P], xg[:, x, 0:D]).then_inc(xgT_psum, 1)
                if up:
                    pe.wait_ge(xgT_ready, n + 1)
                    pe.wait_ge(w_ready, n + 1)
                    if not isinstance(n, int) or n >= 2:
                        pe.wait_ge(hid_e, n - 1)
                    for a in range(2):
                        for m in range(HB):
                            mm = nc.tensor.matmul(ps_s[2 * b + a][:, m * P:(m + 1) * P],
                                                  w_now[:, b, a * H + m * P:a * H + (m + 1) * P], xgT[:, b, :],
                                                  start=True, stop=True)
                        mm.then_inc(up_e, 1)
                    if j == 0:
                        load_experts(r + 1)
                if down:
                    e = experts[j + 1]
                    pe.wait_ge(hid_e, n)
                    if not isinstance(n, int) or n >= 3:
                        pe.wait_ge(y_ready, n - 2)
                    y = ps_o[o][:, 0:D]
                    nc.tensor.matmul(y, ones3[:, :], b2_rows[:, bass.ds(e * D, D)], start=True, stop=False)
                    for m in range(HB):
                        mm = nc.tensor.matmul(y, hid[:, o, m * P:(m + 1) * P],
                                              w_down[:, bass.ds(e, 1), m, :].rearrange("p a n -> p (a n)"),
                                              start=False, stop=(m == HB - 1))
                    mm.then_inc(down_e, 1)

            expert_slots(pe, expert_slot)


_INS = ['L0_attn_tokens', 'L0_attn_wq', 'L0_attn_wk', 'L0_attn_wv', 'L0_attn_wo', 'L0_attn_w_gates', 'L0_attn_rms_w',
        'L0_ffn_Wg', 'L0_ffn_W1', 'L0_ffn_b1', 'L0_ffn_W11', 'L0_ffn_b11', 'L0_ffn_W2', 'L0_ffn_b2',
        'L0_ffn_Ws1', 'L0_ffn_bs1', 'L0_ffn_Ws11', 'L0_ffn_bs11', 'L0_ffn_Ws2', 'L0_ffn_bs2']


def kernel(**inputs):
    import numpy as _np
    import concourse.bacc as _bacc
    from concourse import mybir as _mybir
    from concourse.bass_utils import run_bass_kernel_spmd as _run

    nc = _bacc.Bacc("TRN2", target_bir_lowering=False, num_devices=1)
    arrays, aps = {}, {}
    for name in _INS:
        a = _np.ascontiguousarray(inputs[name])
        arrays[f"in_{name}"] = a
        short = name.replace("L0_attn_", "").replace("L0_ffn_", "")
        aps[short] = nc.dram_tensor(f"in_{name}", a.shape, _mybir.dt.from_np(a.dtype), kind="ExternalInput").ap()
    aps["out"] = nc.dram_tensor("out_0", (1, 2048, 128), _mybir.dt.float32, kind="ExternalOutput").ap()
    attention_moe_layer(nc, **aps)
    r = _run(nc, [arrays], core_ids=[0])
    return r.results[0]["out_0"]
```
